# Optimizing a Trainium2 kernel written in Bass

```python
import numpy as np
import jax
import jax.numpy as jnp

def _softmax(x, axis=-1):
    return jax.nn.softmax(x, axis=axis)

def _gelu(x):
    return jax.nn.gelu(x, approximate=True)

def _silu(x):
    return jax.nn.silu(x)

def _sigmoid(x):
    return jax.nn.sigmoid(x)

def _layernorm(x, axis=-1, eps=1e-05):
    m = jnp.mean(x, axis=axis, keepdims=True)
    v = jnp.var(x, axis=axis, keepdims=True)
    return (x - m) / jnp.sqrt(v + eps)

def _scatter_add(tgt, idx, src, axis=0):
    return tgt.at[idx].add(src)

def _segment_sum(src, seg, n):
    return jax.ops.segment_sum(src, seg, n)
kernel_name = 'mk_xattn_ffn_d2_seqx_r4_1ad2f1'

def setup_inputs(seed: int=0):
    np.random.seed(seed)
    _w = jnp.asarray

    def _rec_inputs():
        import jax
        import jax.numpy as jnp
        _rk = jax.random.key(seed)
        x = 7.22e-05 + 1 * jax.random.normal(jax.random.fold_in(_rk, 1), (32, 256, 256), jnp.float32)
        _lenS = 256 - jax.random.randint(jax.random.fold_in(_rk, 7), (32,), 0, max(1, 256 // 4) + 1, jnp.int32)
        _lenS2 = 77 - jax.random.randint(jax.random.fold_in(_rk, 8), (32,), 0, max(1, 77 // 4) + 1, jnp.int32)
        _ctx_768P = jax.random.normal(jax.random.fold_in(_rk, 11), (32, 16, 192), jnp.float32)
        _ctx_768c = jax.random.dirichlet(jax.random.fold_in(_rk, 511), 0.3 * jnp.ones((16,), jnp.float32), (32, 77))
        _ctx_768t = jnp.einsum('bsk,bkd->bsd', _ctx_768c, _ctx_768P)
        _ctx_768t = _ctx_768t * jax.lax.rsqrt(jnp.mean(jnp.square(_ctx_768t)) + 1e-12) * 0.953939
        ctx_768 = 2.09791e-05 + 1.00001 * (_ctx_768t + 0.3 * jax.random.normal(jax.random.fold_in(_rk, 611), (32, 77, 192), jnp.float32))
        return (x, ctx_768)
    x, ctx_768 = _rec_inputs()

    def _L0_xattn_setup():
        import jax, jax.numpy as jnp
        import numpy as np
        HEADS = 16
        DIM_HEAD = 64
        key = jax.random.key(seed)
        ks = jax.random.split(key, 7)
        B, Nq, Dq = (4, 512, 256)
        Nk, Dc = (256, 192)
        inner = HEADS * DIM_HEAD
        sq = 1.0 / np.sqrt(Dq)
        sc = 1.0 / np.sqrt(Dc)
        si = 1.0 / np.sqrt(inner)
        return {'x': jax.random.normal(ks[0], (B, Nq, Dq), dtype=jnp.float32), 'context': jax.random.normal(ks[1], (B, Nk, Dc), dtype=jnp.float32), 'Wq': jax.random.normal(ks[2], (Dq, inner), dtype=jnp.float32) * sq, 'Wk': jax.random.normal(ks[3], (Dc, inner), dtype=jnp.float32) * sc, 'Wv': jax.random.normal(ks[4], (Dc, inner), dtype=jnp.float32) * sc, 'Wo': jax.random.normal(ks[5], (inner, Dq), dtype=jnp.float32) * si, 'bo': jax.random.normal(ks[6], (Dq,), dtype=jnp.float32) * 0.01}
    _L0_xattn_all = _L0_xattn_setup()
    _L0_xattn_in = {k: v for k, v in _L0_xattn_all.items() if k in ('Wq', 'Wk', 'Wv', 'Wo', 'bo')}
    del _L0_xattn_all

    def _L0_ffn_setup():
        import jax, jax.numpy as jnp
        import numpy as np
        DIM = 256
        HIDDEN = 768
        SCALE = 1.0 / 127.0

        def _dequant(w_int, dtype):
            return w_int.astype(dtype) * jnp.asarray(SCALE, dtype)
        key = jax.random.key(seed)
        k_x, k_g, k_u, k_d = jax.random.split(key, 4)
        x = jax.random.normal(k_x, (4, 512, DIM), dtype=jnp.float32)
        w_gate = jax.random.randint(k_g, (HIDDEN, DIM), -127, 128, dtype=jnp.int32)
        w_up = jax.random.randint(k_u, (HIDDEN, DIM), -127, 128, dtype=jnp.int32)
        w_down = jax.random.randint(k_d, (DIM, HIDDEN), -127, 128, dtype=jnp.int32)
        return {'x': x, 'w_gate': w_gate, 'w_up': w_up, 'w_down': w_down}
    _L0_ffn_all = _L0_ffn_setup()
    _L0_ffn_in = {k: v for k, v in _L0_ffn_all.items() if k in ('w_gate', 'w_up', 'w_down')}
    del _L0_ffn_all

    def _L1_xattn_setup():
        import jax, jax.numpy as jnp
        import numpy as np
        HEADS = 16
        DIM_HEAD = 64
        key = jax.random.key(seed)
        ks = jax.random.split(key, 7)
        b, n, m = (2, 512, 256)
        query_dim, context_dim = (256, 192)
        inner = HEADS * DIM_HEAD
        s_q = 1.0 / np.sqrt(query_dim)
        s_c = 1.0 / np.sqrt(context_dim)
        s_i = 1.0 / np.sqrt(inner)
        return {'x': jax.random.normal(ks[0], (b, n, query_dim), jnp.float32), 'context': jax.random.normal(ks[1], (b, m, context_dim), jnp.float32), 'Wq': jax.random.normal(ks[2], (query_dim, inner), jnp.float32) * s_q, 'Wk': jax.random.normal(ks[3], (context_dim, inner), jnp.float32) * s_c, 'Wv': jax.random.normal(ks[4], (context_dim, inner), jnp.float32) * s_c, 'Wo': jax.random.normal(ks[5], (inner, query_dim), jnp.float32) * s_i, 'bo': jax.random.normal(ks[6], (query_dim,), jnp.float32) * 0.01}
    _L1_xattn_all = _L1_xattn_setup()
    _L1_xattn_in = {k: v for k, v in _L1_xattn_all.items() if k in ('Wq', 'Wk', 'Wv', 'Wo', 'bo')}
    del _L1_xattn_all

    def _L1_ffn_setup():
        import jax, jax.numpy as jnp
        import numpy as np
        INT8_MAX = 127.0

        def _absmax_scale(x, axes):
            amax = jnp.max(jnp.abs(x), axis=axes, keepdims=True)
            return jnp.maximum(amax, 1e-12) / INT8_MAX
        key = jax.random.key(seed)
        k1, k2 = jax.random.split(key)
        lhs = jax.random.normal(k1, (4, 2048, 256), dtype=jnp.float32)
        rhs = jax.random.normal(k2, (256, 256), dtype=jnp.float32)
        return {'lhs': lhs, 'rhs': rhs}
    _L1_ffn_all = _L1_ffn_setup()
    _L1_ffn_in = {k: v for k, v in _L1_ffn_all.items() if k in ('rhs',)}
    del _L1_ffn_all
    return {'x': x, 'ctx_768': ctx_768, 'L0_xattn_Wq': _L0_xattn_in['Wq'], 'L0_xattn_Wk': _L0_xattn_in['Wk'], 'L0_xattn_Wv': _L0_xattn_in['Wv'], 'L0_xattn_Wo': _L0_xattn_in['Wo'], 'L0_xattn_bo': _L0_xattn_in['bo'], 'L0_ffn_w_gate': _L0_ffn_in['w_gate'], 'L0_ffn_w_up': _L0_ffn_in['w_up'], 'L0_ffn_w_down': _L0_ffn_in['w_down'], 'L1_xattn_Wq': _L1_xattn_in['Wq'], 'L1_xattn_Wk': _L1_xattn_in['Wk'], 'L1_xattn_Wv': _L1_xattn_in['Wv'], 'L1_xattn_Wo': _L1_xattn_in['Wo'], 'L1_xattn_bo': _L1_xattn_in['bo'], 'L1_ffn_rhs': _L1_ffn_in['rhs']}

def reference(x, ctx_768, L0_xattn_Wq, L0_xattn_Wk, L0_xattn_Wv, L0_xattn_Wo, L0_xattn_bo, L0_ffn_w_gate, L0_ffn_w_up, L0_ffn_w_down, L1_xattn_Wq, L1_xattn_Wk, L1_xattn_Wv, L1_xattn_Wo, L1_xattn_bo, L1_ffn_rhs):
    import jax
    import jax.numpy as jnp

    def _L0_xattn_ref(x, context, Wq, Wk, Wv, Wo, bo):
        import jax, jax.numpy as jnp
        import numpy as np
        HEADS = 16
        DIM_HEAD = 64
        B, Nq, _ = x.shape
        Nk = context.shape[1]
        h, dh = (HEADS, DIM_HEAD)
        q = (x @ Wq).reshape(B, Nq, h, dh)
        k = (context @ Wk).reshape(B, Nk, h, dh)
        v = (context @ Wv).reshape(B, Nk, h, dh)
        scale = 1.0 / jnp.sqrt(jnp.asarray(dh, dtype=x.dtype))
        scores = jnp.einsum('bqhd,bkhd->bhqk', q, k) * scale
        attn = jax.nn.softmax(scores, axis=-1)
        out = jnp.einsum('bhqk,bkhd->bqhd', attn, v).reshape(B, Nq, h * dh)
        return out @ Wo + bo

    def _L0_ffn_ref(x, w_gate, w_up, w_down):
        import jax, jax.numpy as jnp
        import numpy as np
        DIM = 256
        HIDDEN = 768
        SCALE = 1.0 / 127.0

        def _dequant(w_int, dtype):
            return w_int.astype(dtype) * jnp.asarray(SCALE, dtype)
        wg = _dequant(w_gate, x.dtype)
        wu = _dequant(w_up, x.dtype)
        wd = _dequant(w_down, x.dtype)
        gate = jnp.einsum('bsd,hd->bsh', x, wg)
        up = jnp.einsum('bsd,hd->bsh', x, wu)
        h = jax.nn.silu(gate) * up
        return jnp.einsum('bsh,dh->bsd', h, wd)

    def _L1_xattn_ref(x, context, Wq, Wk, Wv, Wo, bo):
        import jax, jax.numpy as jnp
        import numpy as np
        HEADS = 16
        DIM_HEAD = 64
        b, n, _ = x.shape
        h, d = (HEADS, DIM_HEAD)
        scale = d ** (-0.5)
        q = (x @ Wq).reshape(b, n, h, d).transpose(0, 2, 1, 3)
        k = (context @ Wk).reshape(b, -1, h, d).transpose(0, 2, 1, 3)
        v = (context @ Wv).reshape(b, -1, h, d).transpose(0, 2, 1, 3)
        sim = jnp.einsum('bhid,bhjd->bhij', q, k) * scale
        attn = jax.nn.softmax(sim, axis=-1)
        out = jnp.einsum('bhij,bhjd->bhid', attn, v)
        out = out.transpose(0, 2, 1, 3).reshape(b, n, h * d)
        return out @ Wo + bo

    def _L1_ffn_ref(lhs, rhs):
        import jax, jax.numpy as jnp
        import numpy as np
        INT8_MAX = 127.0

        def _absmax_scale(x, axes):
            amax = jnp.max(jnp.abs(x), axis=axes, keepdims=True)
            return jnp.maximum(amax, 1e-12) / INT8_MAX
        lhs_scale = _absmax_scale(lhs, (2,))
        rhs_scale = _absmax_scale(rhs, (0,))
        q_lhs = jnp.clip(jnp.round(lhs / lhs_scale), -INT8_MAX, INT8_MAX).astype(jnp.int8)
        q_rhs = jnp.clip(jnp.round(rhs / rhs_scale), -INT8_MAX, INT8_MAX).astype(jnp.int8)
        acc = jax.lax.dot_general(q_lhs, q_rhs, (((2,), (0,)), ((), ())), preferred_element_type=jnp.int32)
        return acc.astype(jnp.float32) * lhs_scale * rhs_scale
    x = x + _L0_xattn_ref(_layernorm(x, axis=-1), ctx_768, L0_xattn_Wq, L0_xattn_Wk, L0_xattn_Wv, L0_xattn_Wo, L0_xattn_bo)
    x = x + _L0_ffn_ref(_layernorm(x, axis=-1), L0_ffn_w_gate, L0_ffn_w_up, L0_ffn_w_down)
    x = x + _L1_xattn_ref(_layernorm(x, axis=-1), ctx_768, L1_xattn_Wq, L1_xattn_Wk, L1_xattn_Wv, L1_xattn_Wo, L1_xattn_bo)
    x = x + _L1_ffn_ref(_layernorm(x, axis=-1), L1_ffn_rhs)
    return x

_drawn_inputs = setup_inputs


def setup_inputs(seed=0):
    import zlib

    import numpy as np

    out = dict(_drawn_inputs(seed))
    spreads = {}
    factors = {'L0_xattn_bo': 4.286,
     'L1_xattn_Wq': 8.0,
     'L1_xattn_Wk': 8.0,
     'L1_xattn_Wv': 8.0,
     'L1_xattn_Wo': 8.0,
     'L1_xattn_bo': 8.0,
     'L1_ffn_rhs': 3.421}
    for name, (base, spread) in spreads.items():
        noise = np.random.default_rng([zlib.crc32(name.encode()), seed]).standard_normal(out[name].shape)
        drawn = base * np.exp(spread * noise) if base else spread * noise
        out[name] = jnp.asarray(drawn.astype(out[name].dtype))
    for name, factor in factors.items():
        out[name] = (out[name] * factor).astype(out[name].dtype)
    return out
```

```python
from contextlib import ExitStack

import numpy as np
import concourse.bass as bass
from concourse import mybir

ALU = mybir.AluOpType
ACT = mybir.ActivationFunctionType
F32 = mybir.dt.float32
F32R = mybir.dt.float32r
F16 = mybir.dt.float16
I32 = mybir.dt.int32
AX_X = mybir.AxisListType.X

P = 128
HEADS, DH = 16, 64
UNITS = 4
HPU = HEADS // UNITS
PPU = HPU // 2
EPS = 1e-5
INT8_MAX = 127.0
MAGIC = 1.5 * 2.0 ** 23


def xattn_ffn_kernel(nc, x, ctx, wq0, wk0, wv0, wo0, bo0, w_gate, w_up, w_down,
                     wq1, wk1, wv1, wo1, bo1, rhs, out):
    B, NQ, D = x.shape
    NK, DC = ctx.shape[1], ctx.shape[2]
    INNER = HEADS * DH
    HID = w_gate.shape[0]
    QT = NQ // P
    KT = D // P
    MT = INNER // P
    HC = HID // P
    DCR = DC - P
    TOK = B * NK
    GRP = 352
    NG = TOK // GRP
    SUB = [(0, P), (P, P), (2 * P, GRP - 2 * P)]
    assert NG * GRP == TOK and DCR == 64 and KT == 2 and QT == 2 and HC == 6
    NB = 2 * B
    G_SCALE = 0.5 / INT8_MAX
    FFN_SCALE = 0.5 / INT8_MAX ** 3

    stack = ExitStack()
    with stack:
        def sb(name, shape, dt, where=stack):
            return where.enter_context(nc.sbuf_tensor(name, shape, dt))

        def sem(name):
            return stack.enter_context(nc.semaphore(name))

        keys_d = [nc.dram_tensor(f"keys_{l}", (2, MT, P, TOK), F16).ap() for l in range(2)]
        vals_d = [nc.dram_tensor(f"vals_{l}", (2, TOK, INNER), F16).ap() for l in range(2)]
        mid_d = nc.dram_tensor("mid_x", (B, NQ, D), F32).ap()

        ident = sb("ident", [P, P], F32)
        ident16 = sb("ident16", [P, P], F16)
        half_neg = sb("half_neg", [P, QT], F32)
        eps = sb("eps", [P, QT], F32)
        wq_h = [sb(f"wq_h{l}", [P, KT, INNER], F32R) for l in range(2)]
        wq_l = [sb(f"wq_l{l}", [P, KT, INNER], F32R) for l in range(2)]
        wo_h = [sb(f"wo_h{l}", [P, MT, D], F32R) for l in range(2)]
        wo_l = [sb(f"wo_l{l}", [P, MT, D], F32R) for l in range(2)]
        bo_b = [sb(f"bo_b{l}", [P, D], F32) for l in range(2)]
        wgT = sb("wgT", [P, KT, HID], F32R)
        wuT = sb("wuT", [P, KT, HID], F32R)
        wdT = sb("wdT", [P, HC, D], F32R)
        rhs_q = sb("rhs_q", [P, KT, D], F16)
        rhs_sb = sb("rhs_sb", [P, D], F32)

        psum = stack.enter_context(nc.psum_tensor("psum", [P, 8, 512], F32))

        early = ExitStack()
        raw = sb("raw", [P, 2, INNER], F32, early)
        raw_f = [sb(f"raw_f{i}", [P, HID], F32, early) for i in range(2)]
        r_amax = sb("r_amax", [P, KT], F32, early)
        r_scale = sb("r_scale", [P, KT], F32, early)
        r_inv = sb("r_inv", [P, KT], F32, early)
        r_q = sb("r_q", [P, KT, D], F32, early)
        r_q2 = sb("r_q2", [P, KT, D], F32, early)
        r_sp = sb("r_sp", [P, KT, P], F32, early)
        kf_h = [[sb(f"w{k}{i}_h{l}", [P, INNER], F32R, early) for l in range(2)] for k in "kv" for i in range(2)]
        kf_l = [[sb(f"w{k}{i}_l{l}", [P, INNER], F32R, early) for l in range(2)] for k in "kv" for i in range(2)]
        cx = sb("cx", [P, 3, 2 * P], F32, early)
        c0h = sb("c0h", [P, GRP], F32R, early)
        c0l = sb("c0l", [P, GRP], F32R, early)
        c1 = sb("c1", [P, GRP], F32R, early)
        c1t = sb("c1t", [P, GRP], F32R, early)
        ks = sb("ks", [P, 2, MT, GRP], F16, early)
        vs = sb("vs", [P, 2, 3, INNER], F16, early)

        s_z = sem("s_z")
        s_raw = [sem("s_raw0"), sem("s_raw1")]
        s_wh = sem("s_wh")
        s_wl = sem("s_wl")
        s_int = sem("s_int")
        s_wt = sem("s_wt")
        s_wte = sem("s_wte")
        s_bo = sem("s_bo")
        s_rq = sem("s_rq")
        s_rt = sem("s_rt")

        items = []
        for l, (wk, wv) in enumerate(((wk0, wv0), (wk1, wv1))):
            for k, w in ((0, wk), (2, wv)):
                items.append(([(w[0:P, :], 0, P)], kf_h[k][l][:, :], kf_l[k][l][:, :], 1.0, P))
                items.append(([(w[P:DC, :], 0, DCR), (w[P:DC, :], DCR, DCR)],
                              kf_h[k + 1][l][:, :], kf_l[k + 1][l][0:DCR, :], 1.0, DCR))
        for l, (wq, wo) in enumerate(((wq0, wo0), (wq1, wo1))):
            for k in range(KT):
                items.append(([(wq[k * P:(k + 1) * P, :], 0, P)], wq_h[l][:, k, :], wq_l[l][:, k, :],
                              DH ** -0.5, P))
            for k in range(2):
                src = wo[k * 4 * P:(k + 1) * 4 * P, :].rearrange("(t p) d -> p t d", p=P)
                items.append(([(src, 0, P)], wo_h[l][:, 4 * k:4 * k + 4, :].rearrange("p t d -> p (t d)"),
                              wo_l[l][:, 4 * k:4 * k + 4, :].rearrange("p t d -> p (t d)"), 1.0, P))
        turned = []
        for w, wT in ((w_gate, wgT), (w_up, wuT)):
            for a in range(2):
                src = w[a * 3 * P:(a + 1) * 3 * P, :].rearrange("(t p) d -> p t d", p=P)
                blocks = [(t * D + k * P, k, t) for k in range(KT) for t in range(3)]
                turned.append((src, blocks, [wT[:, k, a * 3 * P:(a + 1) * 3 * P] for k in range(KT)]))
        for a in range(KT):
            src = w_down[a * P:(a + 1) * P, :]
            blocks = [(c * P, c // 3, c % 3) for c in range(HC)]
            turned.append((src, blocks, [wdT[:, 3 * k:3 * k + 3, a * P:(a + 1) * P] for k in range(2)]))
        NI, NT = len(items), len(turned)
        raw_incs = [0, 0]
        raw_need = []
        for j in range(NI + NT + 1):
            raw_incs[j % 2] += 16 * (len(items[j][0]) if j < NI else 1)
            raw_need.append(raw_incs[j % 2])
        RJ = NI + NT

        def raw_free(eng, j):
            if 2 <= j < NI + 2:
                eng.wait_ge(s_wl, j - 1)
            elif j >= NI + 2:
                eng.wait_ge(s_int, j - NI - 1)

        s_cx = sem("s_cx")
        s_ct = sem("s_ct")
        s_ch = sem("s_ch")
        s_cl = sem("s_cl")
        s_kv = sem("s_kv")
        s_kvh = sem("s_kvh")
        s_kvf = sem("s_kvf")
        s_sk = sem("s_sk")
        s_sv = sem("s_sv")
        HALVES = INNER // 512
        KVL = MT + 3 * HALVES
        KVT = 2 * KVL
        RING = 4
        assert KVT % RING == 0

        def kv_tiles():
            for l in range(2):
                for m in range(MT):
                    yield l, "k", m, 0
                for t in range(3):
                    for hf in range(HALVES):
                        yield l, "v", t, hf

        def kv_place(kind, a, b):
            if kind == "k":
                return P, GRP, lambda part: ks[:, part, a, :]
            rows = SUB[a][1]
            return rows, 512, lambda part: vs[0:rows, part, a, b * 512:(b + 1) * 512]

        def staging_free(eng, i, l, kind, a, b):
            if kind == "k" and a == 0:
                eng.wait_ge(s_sk, 16 * 2 * (2 * i + l))
            if kind == "v" and a == 0 and b == 0:
                eng.wait_ge(s_sv, 16 * 6 * (2 * i + l))

        ctx_t = ctx.rearrange("b k c -> (b k) c")

        with nc.Block() as block:
            @block.sync
            def _(sp):
                for j in range(NI + NT + 1):
                    raw_free(sp, j)
                    dst = raw[:, j % 2, :]
                    if j < NI:
                        for src, p0, n in items[j][0]:
                            d = dst[p0:p0 + n, :]
                            if len(src.shape) == 3:
                                d = d.rearrange("p (t d) -> p t d", d=D)
                            sp.dma_start(d, src).then_inc(s_raw[j % 2], 16)
                    elif j < NI + NT:
                        d = dst[:, 0:HID].bitcast(I32)
                        src = turned[j - NI][0]
                        if len(src.shape) == 3:
                            d = d.rearrange("p (t d) -> p t d", d=D)
                        sp.dma_start(d, src).then_inc(s_raw[j % 2], 16)
                    else:
                        d = dst[:, 0:KT * D].rearrange("p (t d) -> p t d", d=D)
                        sp.dma_start(d, rhs.rearrange("(t p) d -> p t d", p=P)).then_inc(s_raw[j % 2], 16)
                for l, bo in enumerate((bo0, bo1)):
                    src = bo.rearrange("(o d) -> o d", o=1).to_broadcast([P, D])
                    sp.dma_start(bo_b[l][:, :], src).then_inc(s_bo, 16)

                def load_group(i):
                    for (t0, n), t in zip(SUB, range(3)):
                        rows = ctx_t[bass.ds(i * GRP + t0, n), :]
                        sp.dma_start(cx[0:n, t, 0:DC], rows).then_inc(s_cx, 16)
                        sp.dma_start(cx[0:n, t, DC:2 * P], rows[:, P:DC]).then_inc(s_cx, 16)

                load_group(0)

                def stores(i):
                    for l in range(2):
                        sp.wait_ge(s_kvf, RING + i * KVT + l * KVL + MT)
                        for part in range(2):
                            sp.dma_start(keys_d[l][part].rearrange("m p t -> p m t")[:, :, bass.ds(i * GRP, GRP)],
                                         ks[:, part, :, :]).then_inc(s_sk, 16)
                        sp.wait_ge(s_kvf, RING + i * KVT + (l + 1) * KVL)
                        for (t0, n), t in zip(SUB, range(3)):
                            for part in range(2):
                                sp.dma_start(vals_d[l][part, bass.ds(i * GRP + t0, n), :],
                                             vs[0:n, part, t, :]).then_inc(s_sv, 16)

                def next_group(i):
                    sp.wait_ge(s_ct, 2 * i + 2)
                    load_group(i + 1)
                    stores(i)

                next_group(0)
                with sp.Fori(1, NG - 1) as i:
                    next_group(i)
                stores(NG - 1)
                sp.wait_ge(s_sk, 16 * 4 * NG)
                sp.wait_ge(s_sv, 16 * 12 * NG)

            @block.gpsimd
            def _(pool):
                pool.memset(ident[:, :], 0.0).then_inc(s_z, 1)
                pool.memset(ident16[:, :], 0.0).then_inc(s_z, 1)
                pool.memset(half_neg[:, :], -0.5).then_inc(s_z, 1)
                pool.memset(eps[:, :], EPS).then_inc(s_z, 1)
                pool.wait_ge(s_z, 4)
                for t in (ident, ident16):
                    pool.affine_select(out=t[:, :], in_=t[:, :], compare_op=ALU.not_equal, fill=1.0, base=0,
                                       pattern=[[-1, P]], channel_multiplier=1).then_inc(s_z, 1)

            @block.scalar
            def _(act):
                for j, (_, hi, lo, scale, rows) in enumerate(items):
                    act.wait_ge(s_raw[j % 2], raw_need[j])
                    act.activation(hi, raw[:, j % 2, :], ACT.Copy, scale=scale).then_inc(s_wh, 1)
                for j, (_, blocks, outs) in enumerate(turned):
                    act.wait_ge(s_wt, j + 1)
                    for k in range(2):
                        o = outs[k]
                        src = psum[:, 2 * (j % 2) + k, 0:3 * P]
                        if len(o.shape) == 3:
                            src = src.rearrange("p (t d) -> p t d", d=P)
                        act.activation(o, src, ACT.Copy).then_inc(s_wte, 1)

                def group(i):
                    act.wait_ge(s_ct, 2 * i + 1)
                    act.wait_ge(s_kv, i * KVT)
                    act.activation(c0h[:, :], psum[:, 0, 0:GRP], ACT.Copy).then_inc(s_ch, 1)
                    act.wait_ge(s_ct, 2 * i + 2)
                    act.activation(c1t[DCR:P, :], psum[DCR:P, 1, 0:GRP], ACT.Copy).then_inc(s_ch, 1)
                    act.activation(c1[0:DCR, :], psum[0:DCR, 1, 0:GRP], ACT.Copy).then_inc(s_ch, 1)
                    for j, (l, kind, a, b) in enumerate(kv_tiles()):
                        rows, cols, place = kv_place(kind, a, b)
                        staging_free(act, i, l, kind, a, b)
                        act.wait_ge(s_kv, i * KVT + j + 1)
                        act.activation(place(0), psum[0:rows, 2 + j % RING, 0:cols], ACT.Copy).then_inc(s_kvh, 1)

                group(0)
                with act.Fori(1, NG) as i:
                    group(i)

            @block.vector
            def _(dve):
                for j, (_, hi, lo, scale, rows) in enumerate(items):
                    dve.wait_ge(s_wh, j + 1)
                    dve.scalar_tensor_tensor(out=lo, in0=raw[0:rows, j % 2, :], scalar=scale,
                                             in1=hi[0:rows, :].bitcast(F32), op0=ALU.mult,
                                             op1=ALU.subtract).then_inc(s_wl, 1)
                for j in range(NT):
                    dve.wait_ge(s_raw[(NI + j) % 2], raw_need[NI + j])
                    if j >= 2:
                        dve.wait_ge(s_wt, j - 1)
                    r = raw_f[j % 2]
                    dve.tensor_copy(r[:, :], raw[:, (NI + j) % 2, 0:HID].bitcast(I32)).then_inc(s_int, 1)
                dve.wait_ge(s_rt, 1)
                rt = psum[:, 4, :].rearrange("p (t d) -> p t d", d=D)
                dve.tensor_reduce(r_amax[:, :], rt, AX_X, ALU.max, apply_absolute_value=True).then_inc(s_rq, 1)
                dve.wait_ge(s_rq, 1)
                dve.tensor_scalar(r_scale[:, :], r_amax[:, :], 1e-12, 1.0 / INT8_MAX, ALU.max, ALU.mult).then_inc(s_rq, 1)
                dve.wait_ge(s_rq, 2)
                dve.reciprocal(r_inv[:, :], r_scale[:, :]).then_inc(s_rq, 1)
                dve.wait_ge(s_rq, 3)
                for t in range(KT):
                    dve.tensor_scalar(r_q[:, t, :], rt[:, t, :], r_inv[:, t:t + 1], INT8_MAX, ALU.mult, ALU.min).then_inc(s_rq, 1)
                dve.wait_ge(s_rq, 5)
                dve.tensor_scalar(r_q2[:, :, :], r_q[:, :, :], -INT8_MAX, MAGIC, ALU.max, ALU.add).then_inc(s_rq, 1)
                dve.wait_ge(s_rq, 6)
                dve.tensor_scalar(r_q[:, :, :], r_q2[:, :, :], MAGIC, None, ALU.subtract).then_inc(s_rq, 1)
                dve.wait_ge(s_z, 6)
                for t in range(KT):
                    dve.tensor_scalar(r_sp[:, t, :], ident[:, :], 0.0, r_scale[:, t:t + 1], ALU.mult, ALU.add).then_inc(s_rq, 1)
                dve.wait_ge(s_rt, 2)
                dve.tensor_copy(rhs_q[:, :, :], psum[:, 5, :].rearrange("p (t d) -> p t d", d=D)).then_inc(s_rq, 1)
                dve.wait_ge(s_rt, 3)
                dve.tensor_copy(rhs_sb[:, :], psum[:, 6, 0:D]).then_inc(s_rq, 1)

                def group(i):
                    dve.wait_ge(s_ch, 3 * i + 1)
                    dve.tensor_tensor(c0l[:, :], psum[:, 0, 0:GRP], c0h[:, :].bitcast(F32),
                                      ALU.subtract).then_inc(s_cl, 1)
                    dve.wait_ge(s_ch, 3 * i + 3)
                    dve.tensor_tensor(c1[DCR:P, :], psum[DCR:P, 1, 0:GRP], c1t[DCR:P, :].bitcast(F32),
                                      ALU.subtract).then_inc(s_cl, 1)
                    for j, (l, kind, a, b) in enumerate(kv_tiles()):
                        rows, cols, place = kv_place(kind, a, b)
                        dve.wait_ge(s_kvh, i * KVT + j + 1)
                        dve.tensor_tensor(place(1), psum[0:rows, 2 + j % RING, 0:cols], place(0),
                                          ALU.subtract).then_inc(s_kvf, 1)

                group(0)
                with dve.Fori(1, NG) as i:
                    group(i)

            @block.tensor
            def _(pe):
                pe.wait_ge(s_z, 6)
                for j, (_, blocks, outs) in enumerate(turned):
                    pe.wait_ge(s_int, j + 1)
                    if j >= 2:
                        pe.wait_ge(s_wte, 2 * (j - 1))
                    for c0, bank, t in blocks:
                        last = pe.transpose(psum[:, 2 * (j % 2) + bank, t * P:(t + 1) * P],
                                            raw_f[j % 2][:, c0:c0 + P], ident[:, :])
                    last.then_inc(s_wt, 1)
                pe.wait_ge(s_raw[RJ % 2], raw_need[RJ])
                for t in range(KT):
                    for k in range(KT):
                        last = pe.transpose(psum[:, 4, t * D + k * P:t * D + (k + 1) * P],
                                            raw[:, RJ % 2, k * D + t * P:k * D + (t + 1) * P], ident[:, :])
                last.then_inc(s_rt, 1)
                pe.wait_ge(s_rq, 7)
                for k in range(KT):
                    for t in range(KT):
                        last = pe.transpose(psum[:, 5, k * D + t * P:k * D + (t + 1) * P],
                                            r_q[:, t, k * P:(k + 1) * P], ident[:, :])
                last.then_inc(s_rt, 1)
                pe.wait_ge(s_rq, 9)
                for t in range(KT):
                    last = pe.transpose(psum[:, 6, t * P:(t + 1) * P], r_sp[:, t, :], ident[:, :])
                last.then_inc(s_rt, 1)
                pe.wait_ge(s_rq, 11)
                pe.wait_ge(s_wte, 2 * NT)
                pe.wait_ge(s_wl, NI)

                def group(i):
                    pe.wait_ge(s_cx, 96 * i + 96)
                    pe.wait_ge(s_cl, 2 * i)
                    for k in range(2):
                        for (t0, n), t in zip(SUB, range(3)):
                            last = pe.transpose(psum[:, k, t0:t0 + n], cx[0:n, t, k * P:(k + 1) * P],
                                                ident[0:n, 0:n])
                        last.then_inc(s_ct, 1)
                    pe.wait_ge(s_cl, 2 * i + 2)
                    for j, (l, kind, a, b) in enumerate(kv_tiles()):
                        rows, cols, _ = kv_place(kind, a, b)
                        pe.wait_ge(s_kvf, i * KVT + j + 1)
                        o = psum[0:rows, 2 + j % RING, 0:cols]
                        if kind == "k":
                            w = slice(a * P, (a + 1) * P)
                            terms = [(kf_h[0][l][:, w], c0h[:, :]), (kf_h[0][l][:, w], c0l[:, :]),
                                     (kf_l[0][l][:, w], c0h[:, :]), (kf_h[1][l][:, w], c1[:, :]),
                                     (kf_l[1][l][0:DCR, w], c1[0:DCR, :])]
                        else:
                            w = slice(b * 512, (b + 1) * 512)
                            ts = slice(SUB[a][0], SUB[a][0] + rows)
                            terms = [(c0h[:, ts], kf_h[2][l][:, w]), (c0l[:, ts], kf_h[2][l][:, w]),
                                     (c0h[:, ts], kf_l[2][l][:, w]), (c1[:, ts], kf_h[3][l][:, w]),
                                     (c1[0:DCR, ts], kf_l[3][l][0:DCR, w])]
                        for q, (lhsT, r) in enumerate(terms):
                            last = pe.matmul(o, lhsT, r, start=(q == 0), stop=(q == len(terms) - 1))
                        last.then_inc(s_kv, 1)

                pe.sem_inc(s_kvf, RING)
                group(0)
                with pe.Fori(1, NG) as i:
                    group(i)
        early.close()

        x_in = sb("x_in", [P, QT, D], F32)
        x_res = sb("x_res", [P, QT, D], F32)
        xn = sb("xn", [P, QT, D], F32)
        xT_h = sb("xT_h", [P, KT, NQ], F32R)
        xT_l = sb("xT_l", [P, KT, NQ], F32R)
        st1 = sb("st1", [P, QT, 6], F32)
        mv1 = sb("mv1", [P, QT, 2], F32)
        rs1 = sb("rs1", [P, QT], F32)
        ve1 = sb("ve1", [P, QT], F32)
        kb = [sb(f"kb{u}", [P, 2, PPU, 2 * NK], F16) for u in range(UNITS)]
        vb = [sb(f"vb{u}", [NK, 2, HPU * DH], F16) for u in range(UNITS)]
        qT_h = sb("qT_h", [P, PPU, NQ], F16)
        qT_l = sb("qT_l", [P, PPU, NQ], F16)
        nmax = sb("nmax", [P, QT, HPU], F32)
        ex = sb("ex", [P, QT, HPU, NK], F32)
        den = sb("den", [P, QT, HPU], F32)
        rden = sb("rden", [P, QT, HPU], F32)
        pr = sb("pr", [P, QT, HPU, NK], F32)
        pT_h = sb("pT_h", [NK, HPU, NQ], F16)
        pT_l = sb("pT_l", [NK, HPU, NQ], F16)
        oT_h = sb("oT_h", [P, PPU, NQ], F32R)
        oT_l = sb("oT_l", [P, PPU, NQ], F32R)
        x1 = sb("x1", [P, QT, D], F32)
        st2 = sb("st2", [P, QT, 6], F32)
        mv2 = sb("mv2", [P, QT, 2], F32)
        rs2 = sb("rs2", [P, QT], F32)
        ve2 = sb("ve2", [P, QT], F32)
        x2 = sb("x2", [P, QT, D], F32)
        x2T_h = sb("x2T_h", [P, KT, NQ], F32R)
        x2T_l = sb("x2T_l", [P, KT, NQ], F32R)
        th = sb("th", [P, 2, NQ], F32)
        sg = sb("sg", [P, 2, NQ], F32)
        hf = sb("hf", [P, 2, NQ], F32)
        hT_h = sb("hT_h", [P, HC, NQ], F32R)
        hT_l = sb("hT_l", [P, HC, NQ], F32R)
        am = sb("am", [P, QT], F32)
        lsc = sb("lsc", [P, QT], F32)
        linv = sb("linv", [P, QT], F32)
        q_a = sb("q_a", [P, QT, D], F32)
        q_b = sb("q_b", [P, QT, D], F32)
        q_i = sb("q_i", [P, QT, D], F16)
        qiT = sb("qiT", [P, KT, NQ], F16)
        ya = sb("ya", [P, QT, D], F32)
        y = sb("y", [P, QT, D], F32)

        SC = psum[:, 0:2, 0:HPU * NK]
        PT = psum[0:NK, 2:4, :].rearrange("p b (h q) -> p b h q", q=NQ)
        OV = psum[:, 4, :].rearrange("p (a q) -> p a q", q=NQ)
        OA = psum[:, 5, :].rearrange("p (t d) -> p t d", d=D)
        RG = [psum[:, 6 + i, :].rearrange("p (a q) -> p a q", q=NQ) for i in range(2)]

        s_kb = [sem(f"s_kb{u}") for u in range(UNITS)]
        s_vb = [sem(f"s_vb{u}") for u in range(UNITS)]
        s_x, s_xr = sem("s_x"), sem("s_xr")
        s_y = sem("s_y")
        s_st, s_mv, s_ve, s_rs, s_xn = (sem(f"s_{a}") for a in ("st", "mv", "ve", "rs", "xn"))
        s_xt, s_xh, s_xl = sem("s_xt"), sem("s_xh"), sem("s_xl")
        s_q, s_qh, s_ql = sem("s_q"), sem("s_qh"), sem("s_ql")
        s_s, s_m, s_e = sem("s_s"), sem("s_m"), sem("s_e")
        s_den, s_r, s_p = sem("s_den"), sem("s_r"), sem("s_p")
        s_t, s_ph, s_pl = sem("s_t"), sem("s_ph"), sem("s_pl")
        s_pv, s_oh, s_ol = sem("s_pv"), sem("s_oh"), sem("s_ol")
        s_oa = sem("s_oa")
        s_xb, s_x1 = sem("s_xb"), sem("s_x1")
        s_st2, s_mv2, s_ve2, s_rs2, s_x2 = (sem(f"s_{a}") for a in ("st2", "mv2", "ve2", "rs2", "x2"))
        s_xt2, s_x2h, s_x2l = sem("s_xt2"), sem("s_x2h"), sem("s_x2l")
        s_g, s_th, s_sg, s_hf, s_hh, s_hl = (sem(f"s_{a}") for a in ("g", "th", "sg", "hf", "hh", "hl"))
        s_d, s_yd = sem("s_d"), sem("s_yd")
        s_am, s_ls, s_li, s_qa, s_qb, s_qi = (sem(f"s_{a}") for a in ("am", "ls", "li", "qa", "qb", "qi"))
        s_qt, s_qe = sem("s_qt"), sem("s_qe")
        s_a1, s_ya = sem("s_a1"), sem("s_ya")
        s_kz = sem("s_kz")

        x_src = [x.rearrange("b (t p) d -> b p t d", p=P), mid_d.rearrange("b (t p) d -> b p t d", p=P)]
        y_dst = [mid_d.rearrange("b (t p) d -> b p t d", p=P), out.rearrange("b (t p) d -> b p t d", p=P)]

        def as_f16(bank):
            return bank[:, 0, :].bitcast(F16).rearrange("p (k q) -> p k q", q=NQ)

        def batch_of(ap, b):
            return ap[bass.ds(b, 1)].rearrange("o p t d -> (o p) t d")

        def bodies(eng, body):
            body(0, None, 0, 0)
            with eng.Fori(1, B - 1) as h:
                body(h, 0, 0, 0)
            body(B - 1, 0, 0, 1)
            body(B, 0, 1, 1)
            with eng.Fori(B + 1, NB - 1) as h:
                body(h, 1, 1, 1)
            body(NB - 1, 1, 1, None)
            body(NB, 1, None, None)

        with nc.Block() as block:
            @block.sync
            def _(sp):
                def load_keys(u, at, l):
                    cols = bass.ds(at, NK)
                    for part in range(2):
                        for a in range(2):
                            src = keys_d[l][part, u * PPU:(u + 1) * PPU, a * DH:(a + 1) * DH].rearrange(
                                "m p k -> p m k")[:, :, cols]
                            sp.dma_start(kb[u][a * DH:(a + 1) * DH, part, :, a * NK:(a + 1) * NK],
                                         src).then_inc(s_kb[u], 16)

                def load_values(u, at, l):
                    src = vals_d[l].rearrange("r k c -> k r c")[bass.ds(at, NK), :,
                                                               u * HPU * DH:(u + 1) * HPU * DH]
                    sp.dma_start(vb[u][:, :, :], src).then_inc(s_vb[u], 16)

                def load_x(dst, s, b, l):
                    sp.dma_start(dst, batch_of(x_src[l], b)).then_inc(s, 16)

                def ready(e):
                    return e if isinstance(e, int) else sp.snap(e)

                sp.sem_inc(s_y, 16)
                sp.wait_ge(s_kz, UNITS)
                load_x(x_in[:, :, :], s_x, 0, 0)
                for u in range(UNITS):
                    load_keys(u, 0, 0)
                for u in range(UNITS - 1):
                    load_values(u, 0, 0)

                def body(h, lt, lh, ln):
                    n = UNITS * h
                    if lt is not None:
                        b_tail = ready(h - 1 - lt * B)
                    if lh is not None:
                        b_own = ready(h - lh * B)
                        at_own = ready((h - lh * B) * NK)
                    if ln is not None:
                        b_next = ready(h + 1 - ln * B)
                        at_next = ready((h + 1 - ln * B) * NK)
                    if lh is not None:
                        if lt is not None:
                            sp.wait_ge(s_pv, n)
                        load_values(UNITS - 1, at_own, lh)
                    for u in range(UNITS):
                        if ln is not None:
                            if u == 0:
                                if ln == 1:
                                    sp.wait_ge(s_y, 16 * (h + 3 - B))
                                sp.wait_ge(s_xn, QT * (h + 1))
                                load_x(x_in[:, :, :], s_x, b_next, ln)
                            sp.wait_ge(s_s, n + u + 1)
                            load_keys(u, at_next, ln)
                            if u > 0:
                                sp.wait_ge(s_pv, n + u)
                                load_values(u - 1, at_next, ln)
                        if u == 1 and lh is not None:
                            if lh == 1:
                                sp.wait_ge(s_y, 16 * (h + 2 - B))
                            if lt is not None:
                                sp.wait_ge(s_x1, h)
                            load_x(x_res[:, :, :], s_xr, b_own, lh)
                    if lt is not None:
                        sp.wait_ge(s_yd, QT * (h + 1))
                        sp.dma_start(batch_of(y_dst[lt], b_tail), y[:, :, :]).then_inc(s_y, 16)

                bodies(sp, body)
                sp.wait_ge(s_y, 16 * (NB + 1))

            @block.tensor
            def _(pe):
                def turn(dst, src):
                    for k in range(KT):
                        for t in range(QT):
                            last = pe.transpose(dst[:, k, t * P:(t + 1) * P], src[:, t, k * P:(k + 1) * P],
                                                (ident if src.dtype == F32 else ident16)[:, :])
                    return last

                def scores(n, u):
                    pe.wait_ge(s_ql, n + 1)
                    pe.wait_ge(s_e, n)
                    for t in range(QT):
                        for a in range(PPU):
                            o = SC[:, t, a * 2 * NK:(a + 1) * 2 * NK]
                            ts = slice(t * P, (t + 1) * P)
                            terms = [(qT_h, 0), (qT_h, 1), (qT_l, 0)]
                            for q, (w, part) in enumerate(terms):
                                last = pe.matmul(o, w[:, a, ts], kb[u][:, part, a, :], start=(q == 0), stop=(q == 2))
                    last.then_inc(s_s, 1)

                def turn_probabilities(n):
                    pe.wait_ge(s_p, n + 1)
                    pe.wait_ge(s_pl, 2 * n)
                    for a in range(PPU):
                        for b in range(2):
                            for t in range(QT):
                                last = pe.transpose(PT[:, a, b, t * P:(t + 1) * P], pr[:, t, 2 * a + b, :],
                                                    ident[:, :])
                        last.then_inc(s_t, 1)

                def queries(n, u, l, o):
                    for a in range(PPU):
                        w = slice((u * PPU + a) * P, (u * PPU + a + 1) * P)
                        terms = [(ww, xx, k) for k in range(KT) for ww, xx in
                                 ((wq_h[l], xT_h), (wq_h[l], xT_l), (wq_l[l], xT_h))]
                        for q, (ww, xx, k) in enumerate(terms):
                            last = pe.matmul(o[:, a, :], ww[:, k, w], xx[:, k, :], start=(q == 0),
                                             stop=(q == len(terms) - 1))
                    last.then_inc(s_q, 1)

                def project(n, u, l):
                    pe.wait_ge(s_ol, n + 1)
                    for t in range(QT):
                        for a in range(PPU):
                            ts, k = slice(t * P, (t + 1) * P), u * PPU + a
                            for q, (oo, ww) in enumerate(((oT_h, wo_h[l]), (oT_l, wo_h[l]), (oT_h, wo_l[l]))):
                                first = u == 0 and t == 0 and a == 0 and q == 0
                                last = pe.matmul(OA[:, t, :], oo[:, a, ts], ww[:, k, :], start=first,
                                                 stop=(u == UNITS - 1 and a == PPU - 1 and q == 2),
                                                 skip_group_check=True)
                    if u == UNITS - 1:
                        last.then_inc(s_oa, 1)

                def weigh_values(n, u, v_need):
                    pe.wait_ge(s_vb[u], v_need)
                    pe.wait_ge(s_ol, n)
                    for a in range(PPU):
                        pe.wait_ge(s_pl, 2 * n + a + 1)
                        for q, (part, pp) in enumerate(((0, pT_h), (0, pT_l), (1, pT_h))):
                            for b in range(2):
                                hd = 2 * a + b
                                last = pe.matmul(OV[b * DH:(b + 1) * DH, a, :], vb[u][:, part, hd * DH:(hd + 1) * DH],
                                                 pp[:, hd, :], start=(q == 0), stop=(q == 2))
                    last.then_inc(s_pv, 1)

                def gate_up(p, c, o):
                    for a, w in ((0, wgT), (1, wuT)):
                        terms = [(k, xx) for k in range(KT) for xx in (x2T_h, x2T_l)]
                        for q, (k, xx) in enumerate(terms):
                            last = pe.matmul(o[:, a, :], w[:, k, c * P:(c + 1) * P], xx[:, k, :], start=(q == 0),
                                             stop=(q == len(terms) - 1))
                    last.then_inc(s_g, 1)

                def down(t, o):
                    terms = [(c, hh) for c in range(HC) for hh in (hT_h, hT_l)]
                    for q, (c, hh) in enumerate(terms):
                        last = pe.matmul(o[:, 0, :], hh[:, c, t * P:(t + 1) * P], wdT[:, c, :], start=(q == 0),
                                         stop=(q == len(terms) - 1))
                    last.then_inc(s_d, 1)

                def quantised(t, o):
                    for k in range(KT):
                        last = pe.matmul(o[:, 0, :], qiT[:, k, t * P:(t + 1) * P], rhs_q[:, k, :], start=(k == 0),
                                         stop=(k == KT - 1))
                    last.then_inc(s_a1, 1)

                pe.sem_inc(s_yd, QT)
                pe.wait_ge(s_xn, QT)
                turn(RG[0], xn).then_inc(s_xt, 1)
                pe.wait_ge(s_xl, 1)
                queries(0, 0, 0, RG[1])

                def body(h, lt, lh, ln):
                    n = UNITS * h
                    held = []

                    def bank(s, value):
                        if len(held) >= 2:
                            pe.wait_ge(*held[-2])
                        elif lt is not None:
                            pe.wait_ge(s_yd, QT * h)
                        held.append((s, value))
                        return RG[(len(held) - 1) % 2]

                    def next_queries(u):
                        if lh is not None and (u < UNITS - 1 or ln is not None):
                            if u == UNITS - 1:
                                pe.wait_ge(s_xl, h + 2)
                            queries(n + u + 1, (u + 1) % UNITS, lh if u < UNITS - 1 else ln,
                                    bank(s_ql, n + u + 2))

                    p = h - 1
                    pf = p
                    if lt == 1:
                        pf = p - B
                    for u in range(UNITS):
                        own = lh if u > 0 else lt
                        if lh is not None:
                            pe.wait_ge(s_kb[u], 64 * (h + 1))
                            scores(n + u, u)
                        if own is not None:
                            turn_probabilities(n + u - 1)
                        if u == 2 and lt == 0:
                            pe.wait_ge(s_x2, QT * (p + 1))
                            turn(bank(s_x2l, pf + 1), x2).then_inc(s_xt2, 1)
                        if u == 2 and lt == 1:
                            pe.wait_ge(s_qi, pf + 1)
                            turn(as_f16(bank(s_qe, pf + 1)), q_i).then_inc(s_qt, 1)
                        next_queries(u)
                        two_back = lh if u > 1 else lt
                        if two_back is not None and not (lt is None and u < 2):
                            project(n + u - 2, (u - 2) % UNITS, two_back)
                        if own is not None:
                            weigh_values(n + u - 1, (u - 1) % UNITS, 16 * ((h if u == 0 else h + 1)))
                        if u == 2 and ln is not None and lh is not None:
                            pe.wait_ge(s_xn, QT * (h + 2))
                            turn(bank(s_xl, h + 2), xn).then_inc(s_xt, 1)
                        if lt == 0 and u >= 2:
                            if u == 2:
                                pe.wait_ge(s_x2l, pf + 1)
                            for c in (range(0, 3) if u == 2 else range(3, HC)):
                                gate_up(p, c, bank(s_hf, HC * pf + c + 1))
                            if u == 3:
                                pe.wait_ge(s_hl, HC * (pf + 1))
                                for t in range(QT):
                                    down(t, bank(s_yd, QT * (p + 1) + t + 1))
                        if lt == 1 and u == 3:
                            pe.wait_ge(s_qe, pf + 1)
                            for t in range(QT):
                                quantised(t, bank(s_ya, QT * pf + t + 1))

                bodies(pe, body)

            @block.scalar
            def _(act):
                def high(dst, src):
                    return act.activation(dst, src, ACT.Copy)

                act.wait_ge(s_xt, 1)
                high(xT_h[:, :, :], RG[0]).then_inc(s_xh, 1)
                act.wait_ge(s_q, 1)
                high(qT_h[:, :, :], RG[1]).then_inc(s_qh, 1)

                def body(h, lt, lh, ln):
                    n, p = UNITS * h, h - 1
                    pf = p - B if lt == 1 else p
                    place = -1

                    def bank():
                        nonlocal place
                        place += 1
                        return RG[place % 2]

                    for u in range(UNITS):
                        own = lh if u > 0 else lt
                        m = n + u - 1
                        if own is not None:
                            act.wait_ge(s_t, 2 * m + 1)
                            high(pT_h[:, 0:2, :], PT[:, 0]).then_inc(s_ph, 1)
                        if lh is not None:
                            act.wait_ge(s_m, n + u + 1)
                            for t in range(QT):
                                for b in range(HPU):
                                    last = act.activation(ex[:, t, b, :], SC[:, t, b * NK:(b + 1) * NK], ACT.Exp,
                                                          bias=nmax[:, t, b:b + 1])
                            last.then_inc(s_e, 1)
                        if own is not None:
                            act.wait_ge(s_t, 2 * m + 2)
                            high(pT_h[:, 2:4, :], PT[:, 1]).then_inc(s_ph, 1)
                        if u == 2 and lt == 0:
                            act.wait_ge(s_xt2, pf + 1)
                            high(x2T_h[:, :, :], bank()).then_inc(s_x2h, 1)
                        if u == 2 and lt == 1:
                            bank()
                        if lh is not None and (u < UNITS - 1 or ln is not None):
                            act.wait_ge(s_q, n + u + 2)
                            high(qT_h[:, :, :], bank()).then_inc(s_qh, 1)
                        if own is not None:
                            act.wait_ge(s_pv, m + 1)
                            high(oT_h[:, :, :], OV).then_inc(s_oh, 1)
                        if u == 2 and ln is not None and lh is not None:
                            act.wait_ge(s_xt, h + 2)
                            high(xT_h[:, :, :], bank()).then_inc(s_xh, 1)
                        if lt == 0 and u >= 2:
                            for c in (range(0, 3) if u == 2 else range(3, HC)):
                                k = HC * pf + c
                                act.wait_ge(s_g, k + 1)
                                act.activation(th[:, c % 2, :], bank()[:, 0, :], ACT.Tanh,
                                               scale=G_SCALE).then_inc(s_th, 1)
                                if c > 0:
                                    act.wait_ge(s_hf, k)
                                    high(hT_h[:, c - 1, :], hf[:, (c - 1) % 2, :]).then_inc(s_hh, 1)
                            if u == 3:
                                act.wait_ge(s_hf, HC * pf + HC)
                                high(hT_h[:, HC - 1, :], hf[:, (HC - 1) % 2, :]).then_inc(s_hh, 1)

                bodies(act, body)

            @block.vector
            def _(dve):
                def low(dst, src, hi):
                    if hi.dtype == F32R:
                        hi = hi.bitcast(F32)
                    return dve.tensor_tensor(dst, src, hi, ALU.subtract)

                def stats(src, st, s_done):
                    for t in range(QT):
                        dve.bn_stats(st[:, t, :], src[:, t, :]).then_inc(s_done, 1)

                def aggregate(st, mv, s_done):
                    for t in range(QT):
                        dve.bn_aggr(mv[:, t, :], st[:, t, :]).then_inc(s_done, 1)

                def normalise(dst, src, mv, rs, s_rs_, s_done, g):
                    dve.wait_ge(s_rs_, g + 1)
                    for t in range(QT):
                        dve.tensor_scalar(dst[:, t, :], src[:, t, :], mv[:, t, 0:1], rs[:, t:t + 1],
                                          ALU.subtract, ALU.mult).then_inc(s_done, 1)

                dve.wait_ge(s_x, 16)
                stats(x_in, st1, s_st)
                dve.wait_ge(s_st, QT)
                aggregate(st1, mv1, s_mv)
                normalise(xn, x_in, mv1, rs1, s_rs, s_xn, 0)
                dve.wait_ge(s_xh, 1)
                low(xT_l[:, :, :], RG[0], xT_h[:, :, :]).then_inc(s_xl, 1)
                dve.wait_ge(s_qh, 1)
                low(qT_l[:, :, :], RG[1], qT_h[:, :, :]).then_inc(s_ql, 1)

                def body(h, lt, lh, ln):
                    n, p = UNITS * h, h - 1
                    pf = p - B if lt == 1 else p
                    place = -1

                    def bank():
                        nonlocal place
                        place += 1
                        return RG[place % 2]

                    for u in range(UNITS):
                        own = lh if u > 0 else lt
                        m = n + u - 1
                        if lh is not None:
                            dve.wait_ge(s_s, n + u + 1)
                            dve.tensor_reduce(nmax[:, :, :], SC.rearrange("p t (h k) -> p t h k", k=NK), AX_X,
                                              ALU.max, negate=True).then_inc(s_m, 1)
                        if own is not None:
                            dve.wait_ge(s_ph, 2 * m + 1)
                            low(pT_l[:, 0:2, :], PT[:, 0], pT_h[:, 0:2, :]).then_inc(s_pl, 1)
                        if u == 1 and lt is not None:
                            dve.wait_ge(s_oa, p + 1)
                            dve.wait_ge(s_xb, p + 1)
                            dve.tensor_tensor(x1[:, :, :], OA, x_res[:, :, :], ALU.add).then_inc(s_x1, 1)
                            dve.wait_ge(s_x1, p + 1)
                            stats(x1, st2, s_st2)
                            if lh is None:
                                dve.wait_ge(s_st2, QT * (p + 1))
                                aggregate(st2, mv2, s_mv2)
                        if lh is not None:
                            if u == 1 and lt is not None:
                                dve.wait_ge(s_st2, QT * (p + 1))
                            dve.wait_ge(s_e, n + u + 1)
                            dve.tensor_reduce(den[:, :, :], ex[:, :, :, :], AX_X, ALU.add).then_inc(s_den, 1)
                            dve.wait_ge(s_den, n + u + 1)
                            dve.reciprocal(rden[:, :, :], den[:, :, :]).then_inc(s_r, 1)
                            if u == 1 and lt is not None:
                                aggregate(st2, mv2, s_mv2)
                        if own is not None:
                            dve.wait_ge(s_ph, 2 * m + 2)
                            low(pT_l[:, 2:4, :], PT[:, 1], pT_h[:, 2:4, :]).then_inc(s_pl, 1)
                        if u == 2 and lt == 0:
                            dve.wait_ge(s_x2h, pf + 1)
                            low(x2T_l[:, :, :], bank(), x2T_h[:, :, :]).then_inc(s_x2l, 1)
                        if u == 2 and lt == 1:
                            dve.wait_ge(s_qt, pf + 1)
                            dve.tensor_copy(qiT[:, :, :], as_f16(bank())).then_inc(s_qe, 1)
                        if lh is not None and (u < UNITS - 1 or ln is not None):
                            dve.wait_ge(s_qh, n + u + 2)
                            low(qT_l[:, :, :], bank(), qT_h[:, :, :]).then_inc(s_ql, 1)
                        if u == 1 and lh is not None and ln is not None:
                            dve.wait_ge(s_x, 16 * (h + 2))
                            stats(x_in, st1, s_st)
                            dve.wait_ge(s_st, QT * (h + 2))
                        if own is not None:
                            dve.wait_ge(s_oh, m + 1)
                            low(oT_l[:, :, :], OV, oT_h[:, :, :]).then_inc(s_ol, 1)
                        if u == 1 and lh is not None and ln is not None:
                            aggregate(st1, mv1, s_mv)
                        if u == 2 and lh is not None and ln is not None:
                            normalise(xn, x_in, mv1, rs1, s_rs, s_xn, h + 1)
                        if u == 1 and lt is not None:
                            normalise(x2, x1, mv2, rs2, s_rs2, s_x2, p)
                            if lt == 1:
                                dve.wait_ge(s_x2, QT * (p + 1))
                                dve.tensor_reduce(am[:, :], x2[:, :, :], AX_X, ALU.max,
                                                  apply_absolute_value=True).then_inc(s_am, 1)
                                dve.wait_ge(s_am, pf + 1)
                                dve.tensor_scalar(lsc[:, :], am[:, :], 1e-12, 1.0 / INT8_MAX, ALU.max,
                                                  ALU.mult).then_inc(s_ls, 1)
                                dve.wait_ge(s_ls, pf + 1)
                                dve.reciprocal(linv[:, :], lsc[:, :]).then_inc(s_li, 1)
                                dve.wait_ge(s_li, pf + 1)
                                for t in range(QT):
                                    dve.tensor_scalar(q_a[:, t, :], x2[:, t, :], linv[:, t:t + 1], INT8_MAX,
                                                      ALU.mult, ALU.min).then_inc(s_qa, 1)
                                dve.wait_ge(s_qa, QT * (pf + 1))
                                dve.tensor_scalar(q_b[:, :, :], q_a[:, :, :], -INT8_MAX, MAGIC, ALU.max,
                                                  ALU.add).then_inc(s_qb, 1)
                                dve.wait_ge(s_qb, pf + 1)
                                dve.tensor_scalar(q_i[:, :, :], q_b[:, :, :], MAGIC, None,
                                                  ALU.subtract).then_inc(s_qi, 1)
                        if u == 2 and ln is not None and lh is not None:
                            dve.wait_ge(s_xh, h + 2)
                            low(xT_l[:, :, :], bank(), xT_h[:, :, :]).then_inc(s_xl, 1)
                        if lt == 0 and u >= 2:
                            for c in (range(0, 3) if u == 2 else range(3, HC)):
                                k = HC * pf + c
                                o = bank()
                                dve.wait_ge(s_th, k + 1)
                                dve.scalar_tensor_tensor(out=sg[:, c % 2, :], in0=th[:, c % 2, :], scalar=1.0,
                                                         in1=o[:, 0, :], op0=ALU.add, op1=ALU.mult).then_inc(s_sg, 1)
                                dve.wait_ge(s_sg, k + 1)
                                if c >= 2:
                                    dve.wait_ge(s_hl, k - 1)
                                dve.tensor_tensor(hf[:, c % 2, :], o[:, 1, :], sg[:, c % 2, :],
                                                  ALU.mult).then_inc(s_hf, 1)
                            if u == 3:
                                dve.wait_ge(s_y, 16 * (p + 1))
                                for t in range(QT):
                                    dve.wait_ge(s_d, QT * pf + t + 1)
                                    dve.scalar_tensor_tensor(out=y[:, t, :], in0=bank()[:, 0, :], scalar=FFN_SCALE,
                                                             in1=x1[:, t, :], op0=ALU.mult,
                                                             op1=ALU.add).then_inc(s_yd, 1)
                        if lt == 1 and u == 3:
                            for t in range(QT):
                                dve.wait_ge(s_a1, QT * pf + t + 1)
                                dve.scalar_tensor_tensor(out=ya[:, t, :], in0=bank()[:, 0, :],
                                                         scalar=lsc[:, t:t + 1], in1=rhs_sb[:, :], op0=ALU.mult,
                                                         op1=ALU.mult).then_inc(s_ya, 1)
                            dve.wait_ge(s_y, 16 * (p + 1))
                            for t in range(QT):
                                dve.wait_ge(s_ya, QT * pf + t + 1)
                                dve.tensor_tensor(y[:, t, :], ya[:, t, :], x1[:, t, :], ALU.add).then_inc(s_yd, 1)

                bodies(dve, body)

            @block.gpsimd
            def _(pool):
                for u in range(UNITS):
                    pool.memset(kb[u][:, :, :, :], 0.0).then_inc(s_kz, 1)

                def inverse_deviation(mv, ve, rs, s_mv_, s_ve_, s_rs_, g):
                    pool.wait_ge(s_mv_, QT * (g + 1))
                    pool.tensor_tensor(ve[:, :], mv[:, :, 1], eps[:, :], ALU.add).then_inc(s_ve_, 1)
                    pool.wait_ge(s_ve_, g + 1)
                    pool.tensor_tensor(rs[:, :], ve[:, :], half_neg[:, :], ALU.pow).then_inc(s_rs_, 1)

                inverse_deviation(mv1, ve1, rs1, s_mv, s_ve, s_rs, 0)

                def body(h, lt, lh, ln):
                    n, p = UNITS * h, h - 1
                    pf = p - B if lt == 1 else p
                    for u in range(UNITS):
                        if u == 1 and lt is not None:
                            inverse_deviation(mv2, ve2, rs2, s_mv2, s_ve2, s_rs2, p)
                        if lh is not None:
                            pool.wait_ge(s_r, n + u + 1)
                            pool.wait_ge(s_t, 2 * (n + u))
                            r = rden[:, :, :].unsqueeze(3).to_broadcast([P, QT, HPU, NK])
                            pool.tensor_tensor(pr[:, :, :, :], ex[:, :, :, :], r, ALU.mult).then_inc(s_p, 1)
                        if u == 1 and lh is not None and ln is not None:
                            inverse_deviation(mv1, ve1, rs1, s_mv, s_ve, s_rs, h + 1)
                        if u == 3 and lh is not None:
                            pool.wait_ge(s_xr, 16 * (h + 1))
                            bias = bo_b[lh][:, :].unsqueeze(1).to_broadcast([P, QT, D])
                            pool.tensor_tensor(x_res[:, :, :], x_res[:, :, :], bias, ALU.add).then_inc(s_xb, 1)
                        if lt == 0 and u >= 2:
                            for c in (range(0, 2) if u == 2 else range(2, HC)):
                                k = HC * pf + c
                                pool.wait_ge(s_hh, k + 1)
                                pool.tensor_tensor(hT_l[:, c, :], hf[:, c % 2, :], hT_h[:, c, :].bitcast(F32),
                                                   ALU.subtract).then_inc(s_hl, 1)

                bodies(pool, body)


_INS = ['x', 'ctx_768', 'L0_xattn_Wq', 'L0_xattn_Wk', 'L0_xattn_Wv', 'L0_xattn_Wo', 'L0_xattn_bo',
        'L0_ffn_w_gate', 'L0_ffn_w_up', 'L0_ffn_w_down', 'L1_xattn_Wq', 'L1_xattn_Wk', 'L1_xattn_Wv',
        'L1_xattn_Wo', 'L1_xattn_bo', 'L1_ffn_rhs']
_OUTS = [((32, 256, 256), 'float32')]


def kernel(**inputs):
    import numpy as _np
    import concourse.bacc as _bacc
    from concourse import mybir as _mybir
    from concourse.bass_utils import run_bass_kernel_spmd as _run

    nc = _bacc.Bacc("TRN2", target_bir_lowering=False, num_devices=1)
    arrays, args = {}, []
    for name in _INS:
        a = _np.ascontiguousarray(inputs[name])
        arrays[f"in_{name}_dram"] = a
        args.append(nc.dram_tensor(f"in_{name}_dram", a.shape, _mybir.dt.from_np(a.dtype), kind="ExternalInput").ap())
    for i, (shape, dtype) in enumerate(_OUTS):
        dt = _mybir.dt.from_np(_np.dtype(dtype))
        args.append(nc.dram_tensor(f"out_{i}_dram", shape, dt, kind="ExternalOutput").ap())
    xattn_ffn_kernel(nc, *args)
    r = _run(nc, [arrays], core_ids=[0])
    return r.results[0]["out_0_dram"]
```

```python
from contextlib import ExitStack

import numpy as np
import concourse.bass as bass
from concourse import mybir

ALU = mybir.AluOpType
ACT = mybir.ActivationFunctionType
F32 = mybir.dt.float32
F32R = mybir.dt.float32r
F16 = mybir.dt.float16
I32 = mybir.dt.int32
AX_X = mybir.AxisListType.X

P = 128
HEADS, DH = 16, 64
UNITS = 4
HPU = HEADS // UNITS
PPU = HPU // 2
EPS = 1e-5
INT8_MAX = 127.0
MAGIC = 1.5 * 2.0 ** 23


def xattn_ffn_kernel(nc, x, ctx, wq0, wk0, wv0, wo0, bo0, w_gate, w_up, w_down,
                     wq1, wk1, wv1, wo1, bo1, rhs, out):
    B, NQ, D = x.shape
    NK, DC = ctx.shape[1], ctx.shape[2]
    INNER = HEADS * DH
    HID = w_gate.shape[0]
    QT = NQ // P
    KT = D // P
    MT = INNER // P
    HC = HID // P
    DCR = DC - P
    TOK = B * NK
    GRP = 352
    NG = TOK // GRP
    SUB = [(0, P), (P, P), (2 * P, GRP - 2 * P)]
    assert NG * GRP == TOK and DCR == 64 and KT == 2 and QT == 2 and HC == 6
    NB = 2 * B
    G_SCALE = 0.5 / INT8_MAX
    FFN_SCALE = 0.5 / INT8_MAX ** 3

    stack = ExitStack()
    with stack:
        def sb(name, shape, dt, where=stack):
            return where.enter_context(nc.sbuf_tensor(name, shape, dt))

        def sem(name):
            return stack.enter_context(nc.semaphore(name))

        keys_d = [nc.dram_tensor(f"keys_{l}", (2, MT, P, TOK), F16).ap() for l in range(2)]
        vals_d = [nc.dram_tensor(f"vals_{l}", (2, TOK, INNER), F16).ap() for l in range(2)]
        mid_d = nc.dram_tensor("mid_x", (B, NQ, D), F32).ap()

        ident = sb("ident", [P, P], F32)
        ident16 = sb("ident16", [P, P], F16)
        half_neg = sb("half_neg", [P, QT], F32)
        eps = sb("eps", [P, QT], F32)
        wq_h = [sb(f"wq_h{l}", [P, KT, INNER], F32R) for l in range(2)]
        wq_l = [sb(f"wq_l{l}", [P, KT, INNER], F32R) for l in range(2)]
        wo_h = [sb(f"wo_h{l}", [P, MT, D], F32R) for l in range(2)]
        wo_l = [sb(f"wo_l{l}", [P, MT, D], F32R) for l in range(2)]
        bo_b = [sb(f"bo_b{l}", [P, D], F32) for l in range(2)]
        wgT = sb("wgT", [P, KT, HID], F32R)
        wuT = sb("wuT", [P, KT, HID], F32R)
        wdT = sb("wdT", [P, HC, D], F32R)
        rhs_q = sb("rhs_q", [P, KT, D], F16)
        rhs_sb = sb("rhs_sb", [P, D], F32)

        psum = stack.enter_context(nc.psum_tensor("psum", [P, 8, 512], F32))

        early = ExitStack()
        raw = sb("raw", [P, 2, INNER], F32, early)
        raw_f = [sb(f"raw_f{i}", [P, HID], F32, early) for i in range(2)]
        r_amax = sb("r_amax", [P, KT], F32, early)
        r_scale = sb("r_scale", [P, KT], F32, early)
        r_inv = sb("r_inv", [P, KT], F32, early)
        r_q = sb("r_q", [P, KT, D], F32, early)
        r_q2 = sb("r_q2", [P, KT, D], F32, early)
        r_sp = sb("r_sp", [P, KT, P], F32, early)
        kf_h = [[sb(f"w{k}{i}_h{l}", [P, INNER], F32R, early) for l in range(2)] for k in "kv" for i in range(2)]
        kf_l = [[sb(f"w{k}{i}_l{l}", [P, INNER], F32R, early) for l in range(2)] for k in "kv" for i in range(2)]
        cx = sb("cx", [P, 3, 2 * P], F32, early)
        c0h = sb("c0h", [P, GRP], F32R, early)
        c0l = sb("c0l", [P, GRP], F32R, early)
        c1 = sb("c1", [P, GRP], F32R, early)
        c1t = sb("c1t", [P, GRP], F32R, early)
        ks = sb("ks", [P, 2, MT, GRP], F16, early)
        vs = sb("vs", [P, 2, 3, INNER], F16, early)

        s_z = sem("s_z")
        s_raw = [sem("s_raw0"), sem("s_raw1")]
        s_wh = sem("s_wh")
        s_wl = sem("s_wl")
        s_int = sem("s_int")
        s_wt = sem("s_wt")
        s_wte = sem("s_wte")
        s_bo = sem("s_bo")
        s_rq = sem("s_rq")
        s_rt = sem("s_rt")

        items = []
        for l, (wk, wv) in enumerate(((wk0, wv0), (wk1, wv1))):
            for k, w in ((0, wk), (2, wv)):
                items.append(([(w[0:P, :], 0, P)], kf_h[k][l][:, :], kf_l[k][l][:, :], 1.0, P))
                items.append(([(w[P:DC, :], 0, DCR), (w[P:DC, :], DCR, DCR)],
                              kf_h[k + 1][l][:, :], kf_l[k + 1][l][0:DCR, :], 1.0, DCR))
        for l, (wq, wo) in enumerate(((wq0, wo0), (wq1, wo1))):
            for k in range(KT):
                items.append(([(wq[k * P:(k + 1) * P, :], 0, P)], wq_h[l][:, k, :], wq_l[l][:, k, :],
                              DH ** -0.5, P))
            for k in range(2):
                src = wo[k * 4 * P:(k + 1) * 4 * P, :].rearrange("(t p) d -> p t d", p=P)
                items.append(([(src, 0, P)], wo_h[l][:, 4 * k:4 * k + 4, :].rearrange("p t d -> p (t d)"),
                              wo_l[l][:, 4 * k:4 * k + 4, :].rearrange("p t d -> p (t d)"), 1.0, P))
        turned = []
        for w, wT in ((w_gate, wgT), (w_up, wuT)):
            for a in range(2):
                src = w[a * 3 * P:(a + 1) * 3 * P, :].rearrange("(t p) d -> p t d", p=P)
                blocks = [(t * D + k * P, k, t) for k in range(KT) for t in range(3)]
                turned.append((src, blocks, [wT[:, k, a * 3 * P:(a + 1) * 3 * P] for k in range(KT)]))
        for a in range(KT):
            src = w_down[a * P:(a + 1) * P, :]
            blocks = [(c * P, c // 3, c % 3) for c in range(HC)]
            turned.append((src, blocks, [wdT[:, 3 * k:3 * k + 3, a * P:(a + 1) * P] for k in range(2)]))
        NI, NT = len(items), len(turned)
        raw_incs = [0, 0]
        raw_need = []
        for j in range(NI + NT + 1):
            raw_incs[j % 2] += 16 * (len(items[j][0]) if j < NI else 1)
            raw_need.append(raw_incs[j % 2])
        RJ = NI + NT

        def raw_free(eng, j):
            if 2 <= j < NI + 2:
                eng.wait_ge(s_wl, j - 1)
            elif j >= NI + 2:
                eng.wait_ge(s_int, j - NI - 1)

        s_cx = sem("s_cx")
        s_ct = sem("s_ct")
        s_ch = sem("s_ch")
        s_cl = sem("s_cl")
        s_kv = sem("s_kv")
        s_kvh = sem("s_kvh")
        s_kvf = sem("s_kvf")
        s_sk = sem("s_sk")
        s_sv = sem("s_sv")
        HALVES = INNER // 512
        KVL = MT + 3 * HALVES
        KVT = 2 * KVL
        RING = 4
        assert KVT % RING == 0

        def kv_tiles():
            for l in range(2):
                for m in range(MT):
                    yield l, "k", m, 0
                for t in range(3):
                    for hf in range(HALVES):
                        yield l, "v", t, hf

        def kv_place(kind, a, b):
            if kind == "k":
                return P, GRP, lambda part: ks[:, part, a, :]
            rows = SUB[a][1]
            return rows, 512, lambda part: vs[0:rows, part, a, b * 512:(b + 1) * 512]

        def staging_free(eng, i, l, kind, a, b):
            if kind == "k" and a == 0:
                eng.wait_ge(s_sk, 16 * 2 * (2 * i + l))
            if kind == "v" and a == 0 and b == 0:
                eng.wait_ge(s_sv, 16 * 6 * (2 * i + l))

        ctx_t = ctx.rearrange("b k c -> (b k) c")

        with nc.Block() as block:
            @block.sync
            def _(sp):
                for j in range(NI + NT + 1):
                    raw_free(sp, j)
                    dst = raw[:, j % 2, :]
                    if j < NI:
                        for src, p0, n in items[j][0]:
                            d = dst[p0:p0 + n, :]
                            if len(src.shape) == 3:
                                d = d.rearrange("p (t d) -> p t d", d=D)
                            sp.dma_start(d, src).then_inc(s_raw[j % 2], 16)
                    elif j < NI + NT:
                        d = dst[:, 0:HID].bitcast(I32)
                        src = turned[j - NI][0]
                        if len(src.shape) == 3:
                            d = d.rearrange("p (t d) -> p t d", d=D)
                        sp.dma_start(d, src).then_inc(s_raw[j % 2], 16)
                    else:
                        d = dst[:, 0:KT * D].rearrange("p (t d) -> p t d", d=D)
                        sp.dma_start(d, rhs.rearrange("(t p) d -> p t d", p=P)).then_inc(s_raw[j % 2], 16)
                for l, bo in enumerate((bo0, bo1)):
                    src = bo.rearrange("(o d) -> o d", o=1).to_broadcast([P, D])
                    sp.dma_start(bo_b[l][:, :], src).then_inc(s_bo, 16)

                def load_group(i):
                    for (t0, n), t in zip(SUB, range(3)):
                        rows = ctx_t[bass.ds(i * GRP + t0, n), :]
                        sp.dma_start(cx[0:n, t, 0:DC], rows).then_inc(s_cx, 16)
                        sp.dma_start(cx[0:n, t, DC:2 * P], rows[:, P:DC]).then_inc(s_cx, 16)

                load_group(0)

                def stores(i):
                    for l in range(2):
                        sp.wait_ge(s_kvf, RING + i * KVT + l * KVL + MT)
                        for part in range(2):
                            sp.dma_start(keys_d[l][part].rearrange("m p t -> p m t")[:, :, bass.ds(i * GRP, GRP)],
                                         ks[:, part, :, :]).then_inc(s_sk, 16)
                        sp.wait_ge(s_kvf, RING + i * KVT + (l + 1) * KVL)
                        for (t0, n), t in zip(SUB, range(3)):
                            for part in range(2):
                                sp.dma_start(vals_d[l][part, bass.ds(i * GRP + t0, n), :],
                                             vs[0:n, part, t, :]).then_inc(s_sv, 16)

                def next_group(i):
                    sp.wait_ge(s_ct, 2 * i + 2)
                    load_group(i + 1)
                    stores(i)

                next_group(0)
                with sp.Fori(1, NG - 1) as i:
                    next_group(i)
                stores(NG - 1)
                sp.wait_ge(s_sk, 16 * 4 * NG)
                sp.wait_ge(s_sv, 16 * 12 * NG)

            @block.gpsimd
            def _(pool):
                pool.memset(ident[:, :], 0.0).then_inc(s_z, 1)
                pool.memset(ident16[:, :], 0.0).then_inc(s_z, 1)
                pool.memset(half_neg[:, :], -0.5).then_inc(s_z, 1)
                pool.memset(eps[:, :], EPS).then_inc(s_z, 1)
                pool.wait_ge(s_z, 4)
                for t in (ident, ident16):
                    pool.affine_select(out=t[:, :], in_=t[:, :], compare_op=ALU.not_equal, fill=1.0, base=0,
                                       pattern=[[-1, P]], channel_multiplier=1).then_inc(s_z, 1)

            @block.scalar
            def _(act):
                for j, (_, hi, lo, scale, rows) in enumerate(items):
                    act.wait_ge(s_raw[j % 2], raw_need[j])
                    act.activation(hi, raw[:, j % 2, :], ACT.Copy, scale=scale).then_inc(s_wh, 1)
                for j, (_, blocks, outs) in enumerate(turned):
                    act.wait_ge(s_wt, j + 1)
                    for k in range(2):
                        o = outs[k]
                        src = psum[:, 2 * (j % 2) + k, 0:3 * P]
                        if len(o.shape) == 3:
                            src = src.rearrange("p (t d) -> p t d", d=P)
                        act.activation(o, src, ACT.Copy).then_inc(s_wte, 1)

                def group(i):
                    act.wait_ge(s_ct, 2 * i + 1)
                    act.wait_ge(s_kv, i * KVT)
                    act.activation(c0h[:, :], psum[:, 0, 0:GRP], ACT.Copy).then_inc(s_ch, 1)
                    act.wait_ge(s_ct, 2 * i + 2)
                    act.activation(c1t[DCR:P, :], psum[DCR:P, 1, 0:GRP], ACT.Copy).then_inc(s_ch, 1)
                    act.activation(c1[0:DCR, :], psum[0:DCR, 1, 0:GRP], ACT.Copy).then_inc(s_ch, 1)
                    for j, (l, kind, a, b) in enumerate(kv_tiles()):
                        rows, cols, place = kv_place(kind, a, b)
                        staging_free(act, i, l, kind, a, b)
                        act.wait_ge(s_kv, i * KVT + j + 1)
                        act.activation(place(0), psum[0:rows, 2 + j % RING, 0:cols], ACT.Copy).then_inc(s_kvh, 1)

                group(0)
                with act.Fori(1, NG) as i:
                    group(i)

            @block.vector
            def _(dve):
                for j, (_, hi, lo, scale, rows) in enumerate(items):
                    dve.wait_ge(s_wh, j + 1)
                    dve.scalar_tensor_tensor(out=lo, in0=raw[0:rows, j % 2, :], scalar=scale,
                                             in1=hi[0:rows, :].bitcast(F32), op0=ALU.mult,
                                             op1=ALU.subtract).then_inc(s_wl, 1)
                for j in range(NT):
                    dve.wait_ge(s_raw[(NI + j) % 2], raw_need[NI + j])
                    if j >= 2:
                        dve.wait_ge(s_wt, j - 1)
                    r = raw_f[j % 2]
                    dve.tensor_copy(r[:, :], raw[:, (NI + j) % 2, 0:HID].bitcast(I32)).then_inc(s_int, 1)
                dve.wait_ge(s_rt, 1)
                rt = psum[:, 4, :].rearrange("p (t d) -> p t d", d=D)
                dve.tensor_reduce(r_amax[:, :], rt, AX_X, ALU.max, apply_absolute_value=True).then_inc(s_rq, 1)
                dve.wait_ge(s_rq, 1)
                dve.tensor_scalar(r_scale[:, :], r_amax[:, :], 1e-12, 1.0 / INT8_MAX, ALU.max, ALU.mult).then_inc(s_rq, 1)
                dve.wait_ge(s_rq, 2)
                dve.reciprocal(r_inv[:, :], r_scale[:, :]).then_inc(s_rq, 1)
                dve.wait_ge(s_rq, 3)
                for t in range(KT):
                    dve.tensor_scalar(r_q[:, t, :], rt[:, t, :], r_inv[:, t:t + 1], INT8_MAX, ALU.mult, ALU.min).then_inc(s_rq, 1)
                dve.wait_ge(s_rq, 5)
                dve.tensor_scalar(r_q2[:, :, :], r_q[:, :, :], -INT8_MAX, MAGIC, ALU.max, ALU.add).then_inc(s_rq, 1)
                dve.wait_ge(s_rq, 6)
                dve.tensor_scalar(r_q[:, :, :], r_q2[:, :, :], MAGIC, None, ALU.subtract).then_inc(s_rq, 1)
                dve.wait_ge(s_z, 6)
                for t in range(KT):
                    dve.tensor_scalar(r_sp[:, t, :], ident[:, :], 0.0, r_scale[:, t:t + 1], ALU.mult, ALU.add).then_inc(s_rq, 1)
                dve.wait_ge(s_rt, 2)
                dve.tensor_copy(rhs_q[:, :, :], psum[:, 5, :].rearrange("p (t d) -> p t d", d=D)).then_inc(s_rq, 1)
                dve.wait_ge(s_rt, 3)
                dve.tensor_copy(rhs_sb[:, :], psum[:, 6, 0:D]).then_inc(s_rq, 1)

                def group(i):
                    dve.wait_ge(s_ch, 3 * i + 1)
                    dve.tensor_tensor(c0l[:, :], psum[:, 0, 0:GRP], c0h[:, :].bitcast(F32),
                                      ALU.subtract).then_inc(s_cl, 1)
                    dve.wait_ge(s_ch, 3 * i + 3)
                    dve.tensor_tensor(c1[DCR:P, :], psum[DCR:P, 1, 0:GRP], c1t[DCR:P, :].bitcast(F32),
                                      ALU.subtract).then_inc(s_cl, 1)
                    for j, (l, kind, a, b) in enumerate(kv_tiles()):
                        rows, cols, place = kv_place(kind, a, b)
                        dve.wait_ge(s_kvh, i * KVT + j + 1)
                        dve.tensor_tensor(place(1), psum[0:rows, 2 + j % RING, 0:cols], place(0),
                                          ALU.subtract).then_inc(s_kvf, 1)

                group(0)
                with dve.Fori(1, NG) as i:
                    group(i)

            @block.tensor
            def _(pe):
                pe.wait_ge(s_z, 6)
                for j, (_, blocks, outs) in enumerate(turned):
                    pe.wait_ge(s_int, j + 1)
                    if j >= 2:
                        pe.wait_ge(s_wte, 2 * (j - 1))
                    for c0, bank, t in blocks:
                        last = pe.transpose(psum[:, 2 * (j % 2) + bank, t * P:(t + 1) * P],
                                            raw_f[j % 2][:, c0:c0 + P], ident[:, :])
                    last.then_inc(s_wt, 1)
                pe.wait_ge(s_raw[RJ % 2], raw_need[RJ])
                for t in range(KT):
                    for k in range(KT):
                        last = pe.transpose(psum[:, 4, t * D + k * P:t * D + (k + 1) * P],
                                            raw[:, RJ % 2, k * D + t * P:k * D + (t + 1) * P], ident[:, :])
                last.then_inc(s_rt, 1)
                pe.wait_ge(s_rq, 7)
                for k in range(KT):
                    for t in range(KT):
                        last = pe.transpose(psum[:, 5, k * D + t * P:k * D + (t + 1) * P],
                                            r_q[:, t, k * P:(k + 1) * P], ident[:, :])
                last.then_inc(s_rt, 1)
                pe.wait_ge(s_rq, 9)
                for t in range(KT):
                    last = pe.transpose(psum[:, 6, t * P:(t + 1) * P], r_sp[:, t, :], ident[:, :])
                last.then_inc(s_rt, 1)
                pe.wait_ge(s_rq, 11)
                pe.wait_ge(s_wte, 2 * NT)
                pe.wait_ge(s_wl, NI)

                def group(i):
                    pe.wait_ge(s_cx, 96 * i + 96)
                    pe.wait_ge(s_cl, 2 * i)
                    for k in range(2):
                        for (t0, n), t in zip(SUB, range(3)):
                            last = pe.transpose(psum[:, k, t0:t0 + n], cx[0:n, t, k * P:(k + 1) * P],
                                                ident[0:n, 0:n])
                        last.then_inc(s_ct, 1)
                    pe.wait_ge(s_cl, 2 * i + 2)
                    for j, (l, kind, a, b) in enumerate(kv_tiles()):
                        rows, cols, _ = kv_place(kind, a, b)
                        pe.wait_ge(s_kvf, i * KVT + j + 1)
                        o = psum[0:rows, 2 + j % RING, 0:cols]
                        if kind == "k":
                            w = slice(a * P, (a + 1) * P)
                            terms = [(kf_h[0][l][:, w], c0h[:, :]), (kf_h[0][l][:, w], c0l[:, :]),
                                     (kf_l[0][l][:, w], c0h[:, :]), (kf_h[1][l][:, w], c1[:, :]),
                                     (kf_l[1][l][0:DCR, w], c1[0:DCR, :])]
                        else:
                            w = slice(b * 512, (b + 1) * 512)
                            ts = slice(SUB[a][0], SUB[a][0] + rows)
                            terms = [(c0h[:, ts], kf_h[2][l][:, w]), (c0l[:, ts], kf_h[2][l][:, w]),
                                     (c0h[:, ts], kf_l[2][l][:, w]), (c1[:, ts], kf_h[3][l][:, w]),
                                     (c1[0:DCR, ts], kf_l[3][l][0:DCR, w])]
                        for q, (lhsT, r) in enumerate(terms):
                            last = pe.matmul(o, lhsT, r, start=(q == 0), stop=(q == len(terms) - 1))
                        last.then_inc(s_kv, 1)

                pe.sem_inc(s_kvf, RING)
                group(0)
                with pe.Fori(1, NG) as i:
                    group(i)
        early.close()

        x_in = sb("x_in", [P, QT, D], F32)
        x_res = sb("x_res", [P, QT, D], F32)
        xn = sb("xn", [P, QT, D], F32)
        xT_h = sb("xT_h", [P, KT, NQ], F32R)
        xT_l = sb("xT_l", [P, KT, NQ], F32R)
        st1 = sb("st1", [P, QT, 6], F32)
        mv1 = sb("mv1", [P, QT, 2], F32)
        rs1 = sb("rs1", [P, QT], F32)
        ve1 = sb("ve1", [P, QT], F32)
        kb = [sb(f"kb{u}", [P, 2, PPU, 2 * NK], F16) for u in range(UNITS)]
        vb = [sb(f"vb{u}", [NK, 2, HPU * DH], F16) for u in range(UNITS)]
        qT_h = sb("qT_h", [P, PPU, NQ], F16)
        qT_l = sb("qT_l", [P, PPU, NQ], F16)
        nmax = sb("nmax", [P, QT, HPU], F32)
        ex = sb("ex", [P, QT, HPU, NK], F32)
        den = sb("den", [P, QT, HPU], F32)
        rden = sb("rden", [P, QT, HPU], F32)
        pr = sb("pr", [P, QT, HPU, NK], F32)
        pT_h = sb("pT_h", [NK, HPU, NQ], F16)
        pT_l = sb("pT_l", [NK, HPU, NQ], F16)
        oT_h = sb("oT_h", [P, PPU, NQ], F32R)
        oT_l = sb("oT_l", [P, PPU, NQ], F32R)
        x1 = sb("x1", [P, QT, D], F32)
        st2 = sb("st2", [P, QT, 6], F32)
        mv2 = sb("mv2", [P, QT, 2], F32)
        rs2 = sb("rs2", [P, QT], F32)
        ve2 = sb("ve2", [P, QT], F32)
        x2 = sb("x2", [P, QT, D], F32)
        x2T_h = sb("x2T_h", [P, KT, NQ], F32R)
        x2T_l = sb("x2T_l", [P, KT, NQ], F32R)
        th = sb("th", [P, 2, NQ], F32)
        sg = sb("sg", [P, 2, NQ], F32)
        hf = sb("hf", [P, 2, NQ], F32)
        hT_h = sb("hT_h", [P, HC, NQ], F32R)
        hT_l = sb("hT_l", [P, HC, NQ], F32R)
        am = sb("am", [P, QT], F32)
        lsc = sb("lsc", [P, QT], F32)
        linv = sb("linv", [P, QT], F32)
        q_a = sb("q_a", [P, QT, D], F32)
        q_b = sb("q_b", [P, QT, D], F32)
        q_i = sb("q_i", [P, QT, D], F16)
        qiT = sb("qiT", [P, KT, NQ], F16)
        ya = sb("ya", [P, QT, D], F32)
        y = sb("y", [P, QT, D], F32)

        SC = psum[:, 0:2, 0:HPU * NK]
        PT = psum[0:NK, 2:4, :].rearrange("p b (h q) -> p b h q", q=NQ)
        OV = psum[:, 4, :].rearrange("p (a q) -> p a q", q=NQ)
        OA = psum[:, 5, :].rearrange("p (t d) -> p t d", d=D)
        RG = [psum[:, 6 + i, :].rearrange("p (a q) -> p a q", q=NQ) for i in range(2)]

        s_kb = [sem(f"s_kb{u}") for u in range(UNITS)]
        s_vb = [sem(f"s_vb{u}") for u in range(UNITS)]
        s_x, s_xr = sem("s_x"), sem("s_xr")
        s_y = sem("s_y")
        s_st, s_mv, s_ve, s_rs, s_xn = (sem(f"s_{a}") for a in ("st", "mv", "ve", "rs", "xn"))
        s_xt, s_xh, s_xl = sem("s_xt"), sem("s_xh"), sem("s_xl")
        s_q, s_qh, s_ql = sem("s_q"), sem("s_qh"), sem("s_ql")
        s_s, s_m, s_e = sem("s_s"), sem("s_m"), sem("s_e")
        s_den, s_r, s_p = sem("s_den"), sem("s_r"), sem("s_p")
        s_t, s_ph, s_pl = sem("s_t"), sem("s_ph"), sem("s_pl")
        s_pv, s_oh, s_ol = sem("s_pv"), sem("s_oh"), sem("s_ol")
        s_oa = sem("s_oa")
        s_xb, s_x1 = sem("s_xb"), sem("s_x1")
        s_st2, s_mv2, s_ve2, s_rs2, s_x2 = (sem(f"s_{a}") for a in ("st2", "mv2", "ve2", "rs2", "x2"))
        s_xt2, s_x2h, s_x2l = sem("s_xt2"), sem("s_x2h"), sem("s_x2l")
        s_g, s_th, s_sg, s_hf, s_hh, s_hl = (sem(f"s_{a}") for a in ("g", "th", "sg", "hf", "hh", "hl"))
        s_d, s_yd = sem("s_d"), sem("s_yd")
        s_am, s_ls, s_li, s_qa, s_qb, s_qi = (sem(f"s_{a}") for a in ("am", "ls", "li", "qa", "qb", "qi"))
        s_yx, s_yq = sem("s_yx"), sem("s_yq")
        s_qt, s_qe = sem("s_qt"), sem("s_qe")
        s_a1, s_ya = sem("s_a1"), sem("s_ya")
        s_kz = sem("s_kz")

        x_src = [x.rearrange("b (t p) d -> b p t d", p=P), mid_d.rearrange("b (t p) d -> b p t d", p=P)]
        y_dst = [mid_d.rearrange("b (t p) d -> b p t d", p=P), out.rearrange("b (t p) d -> b p t d", p=P)]

        def as_f16(bank):
            return bank[:, 0, :].bitcast(F16).rearrange("p (k q) -> p k q", q=NQ)

        def batch_of(ap, b):
            return ap[bass.ds(b, 1)].rearrange("o p t d -> (o p) t d")

        def layer_of(g):
            return None if g < 0 or g >= NB else g // B

        def uses(l2, l1, l0, ln):
            out = []
            for u in range(UNITS):
                if l0 is not None and (u < UNITS - 1 or ln is not None):
                    out.append(("q", u))
                if l2 == 0:
                    out += [[("gu", 1), ("gu", 2)], [("gu", 3), ("gu", 4)], [], [("down", 0)]][u]
                if l2 == 1:
                    out += [[], [("turned_q", 0), ("down", 0), ("down", 1)], [], []][u]
                if u == 2:
                    if l0 is not None and ln is not None:
                        out.append(("turned_x", 0))
                    if l2 == 0:
                        out.append(("gu", 5))
                if u == 3:
                    if l1 == 0:
                        out.append(("turned_x2", 0))
                    if l2 == 0:
                        out.append(("down", 1))
                    if l1 == 0:
                        out.append(("gu", 0))
            return out

        def released(use, h, l2, l1):
            kind, k = use
            if kind == "q":
                return s_ql, UNITS * h + k + 2
            if kind == "turned_x":
                return s_xl, h + 2
            if kind == "turned_x2":
                return s_x2l, h
            if kind == "turned_q":
                return s_qe, h - 1 - B
            if kind == "gu":
                return s_hf, HC * (h - 1 if k == 0 else h - 2) + k + 1
            if l2 == 0:
                return s_yd, QT * (h - 2) + k + 1
            return s_ya, QT * (h - 2 - B) + k + 1

        kinds, gu0 = {}, None
        ring = [(("turned_x", 0), -1), (("q", UNITS - 1), -1)]
        place = 0
        for h in range(NB + 2):
            ls = tuple(layer_of(h + d) for d in (-2, -1, 0, 1))
            plan, here = {}, []
            for q, use in enumerate(uses(*ls)):
                before = (ring + here)[-2]
                plan[use] = ((place + q) % 2, before)
                here.append((use, 0))
            place += len(here)
            ring = [(use, d - 1) for use, d in (ring + here)[-2:]]
            kinds[h] = (ls, plan, gu0)
            gu0 = plan[("gu", 0)][0] if ("gu", 0) in plan else None
        for loop in (range(3, B - 1), range(B + 3, NB - 1)):
            assert all(kinds[h] == kinds[loop[0]] for h in loop)

        def bodies(eng, body):
            def one(h, like):
                ls, plan, gu0 = kinds[like]
                body(h, plan, like, gu0, *ls)

            for first, last in ((3, B - 1), (B + 3, NB - 1)):
                for h in range(first - 3, first):
                    one(h, h)
                with eng.Fori(first, last) as h:
                    one(h, first)
                one(last, last)
            one(NB, NB)
            one(NB + 1, NB + 1)

        with nc.Block() as block:
            @block.sync
            def _(sp):
                def load_keys(u, at, l):
                    cols = bass.ds(at, NK)
                    for part in range(2):
                        for a in range(2):
                            src = keys_d[l][part, u * PPU:(u + 1) * PPU, a * DH:(a + 1) * DH].rearrange(
                                "m p k -> p m k")[:, :, cols]
                            sp.dma_start(kb[u][a * DH:(a + 1) * DH, part, :, a * NK:(a + 1) * NK],
                                         src).then_inc(s_kb[u], 16)

                def load_values(u, at, l):
                    src = vals_d[l].rearrange("r k c -> k r c")[bass.ds(at, NK), :,
                                                               u * HPU * DH:(u + 1) * HPU * DH]
                    sp.dma_start(vb[u][:, :, :], src).then_inc(s_vb[u], 16)

                def load_x(dst, s, b, l):
                    sp.dma_start(dst, batch_of(x_src[l], b)).then_inc(s, 16)

                def ready(e):
                    return e if isinstance(e, int) else sp.snap(e)

                sp.sem_inc(s_y, 16)
                load_x(x_in[:, :, :], s_x, 0, 0)
                sp.wait_ge(s_kz, UNITS)
                for u in range(UNITS):
                    load_keys(u, 0, 0)
                for u in range(UNITS - 2):
                    load_values(u, 0, 0)

                def body(h, plan, like, gu0, l2, l1, l0, ln):
                    n = UNITS * h
                    if l2 is not None:
                        b_out = ready(h - 2 - l2 * B)
                    if l0 is not None:
                        b_own = ready(h - l0 * B)
                        at_own = ready((h - l0 * B) * NK)
                    if ln is not None:
                        b_next = ready(h + 1 - ln * B)
                        at_next = ready((h + 1 - ln * B) * NK)
                    for u in range(UNITS):
                        if l0 is not None and ln is not None:
                            if u == 0:
                                if ln == 1:
                                    sp.wait_ge(s_y, 16 * (h + 3 - B))
                                sp.wait_ge(s_xn, QT * (h + 1))
                                load_x(x_in[:, :, :], s_x, b_next, ln)
                        if l0 is not None and u < 2:
                            if l1 is not None:
                                sp.wait_ge(s_pv, n + u - 1)
                            load_values(u + 2, at_own, l0)
                        if l0 is not None and ln is not None:
                            sp.wait_ge(s_s, n + u + 1)
                            load_keys(u, at_next, ln)
                            if u >= 2:
                                sp.wait_ge(s_pv, n + u - 1)
                                load_values(u - 2, at_next, ln)
                        if u == 3 and l0 is not None:
                            if l0 == 1:
                                sp.wait_ge(s_y, 16 * (h + 2 - B))
                            if l1 is not None:
                                sp.wait_ge(s_x1, h)
                            load_x(x_res[:, :, :], s_xr, b_own, l0)
                        if (u == 3 and l2 == 0) or (u == 2 and l2 == 1):
                            sp.wait_ge(*((s_yd, QT * (h - 1)) if l2 == 0 else (s_yq, h - 1 - B)))
                            sp.dma_start(batch_of(y_dst[l2], b_out), y[:, :, :]).then_inc(s_y, 16)

                bodies(sp, body)
                sp.wait_ge(s_y, 16 * (NB + 1))

            @block.tensor
            def _(pe):
                def turn(dst, src):
                    for k in range(KT):
                        for t in range(QT):
                            last = pe.transpose(dst[:, k, t * P:(t + 1) * P], src[:, t, k * P:(k + 1) * P],
                                                (ident if src.dtype == F32 else ident16)[:, :])
                    return last

                def scores(n, u, k_need):
                    pe.wait_ge(s_ql, n + 1)
                    pe.wait_ge(s_kb[u], k_need)
                    for t in range(QT):
                        if not (isinstance(n, int) and n == 0):
                            pe.wait_ge(s_e, QT * (n - 1) + t + 1)
                        for a in range(PPU):
                            o = SC[:, t, a * 2 * NK:(a + 1) * 2 * NK]
                            ts = slice(t * P, (t + 1) * P)
                            for q, (w, part) in enumerate(((qT_h, 0), (qT_h, 1), (qT_l, 0))):
                                last = pe.matmul(o, w[:, a, ts], kb[u][:, part, a, :], start=(q == 0), stop=(q == 2))
                    last.then_inc(s_s, 1)

                def turn_probabilities(n):
                    pe.wait_ge(s_p, n + 1)
                    pe.wait_ge(s_pl, 2 * n)
                    for a in range(PPU):
                        for b in range(2):
                            for t in range(QT):
                                last = pe.transpose(PT[:, a, b, t * P:(t + 1) * P], pr[:, t, 2 * a + b, :],
                                                    ident[:, :])
                        last.then_inc(s_t, 1)

                def queries(u, l, o):
                    for a in range(PPU):
                        w = slice((u * PPU + a) * P, (u * PPU + a + 1) * P)
                        terms = [(ww, xx, k) for k in range(KT) for ww, xx in
                                 ((wq_h[l], xT_h), (wq_h[l], xT_l), (wq_l[l], xT_h))]
                        for q, (ww, xx, k) in enumerate(terms):
                            last = pe.matmul(o[:, a, :], ww[:, k, w], xx[:, k, :], start=(q == 0),
                                             stop=(q == len(terms) - 1))
                    last.then_inc(s_q, 1)

                def project(n, u, l):
                    pe.wait_ge(s_ol, n + 1)
                    for t in range(QT):
                        for a in range(PPU):
                            ts, k = slice(t * P, (t + 1) * P), u * PPU + a
                            for q, (oo, ww) in enumerate(((oT_h, wo_h[l]), (oT_l, wo_h[l]), (oT_h, wo_l[l]))):
                                first = u == 0 and t == 0 and a == 0 and q == 0
                                last = pe.matmul(OA[:, t, :], oo[:, a, ts], ww[:, k, :], start=first,
                                                 stop=(u == UNITS - 1 and a == PPU - 1 and q == 2),
                                                 skip_group_check=True)
                    if u == UNITS - 1:
                        last.then_inc(s_oa, 1)

                def weigh_values(n, u, v_need):
                    pe.wait_ge(s_vb[u], v_need)
                    if not (isinstance(n, int) and n == 0):
                        pe.wait_ge(s_ol, n)
                    for a in range(PPU):
                        pe.wait_ge(s_pl, 2 * n + a + 1)
                        for q, (part, pp) in enumerate(((0, pT_h), (0, pT_l), (1, pT_h))):
                            for b in range(2):
                                hd = 2 * a + b
                                last = pe.matmul(OV[b * DH:(b + 1) * DH, a, :], vb[u][:, part, hd * DH:(hd + 1) * DH],
                                                 pp[:, hd, :], start=(q == 0), stop=(q == 2))
                    last.then_inc(s_pv, 1)

                def gate_up(c, o):
                    for a, w in ((0, wgT), (1, wuT)):
                        terms = [(k, xx) for k in range(KT) for xx in (x2T_h, x2T_l)]
                        for q, (k, xx) in enumerate(terms):
                            last = pe.matmul(o[:, a, :], w[:, k, c * P:(c + 1) * P], xx[:, k, :], start=(q == 0),
                                             stop=(q == len(terms) - 1))
                    last.then_inc(s_g, 1)

                def down(t, o):
                    terms = [(c, hh) for c in range(HC) for hh in (hT_h, hT_l)]
                    for q, (c, hh) in enumerate(terms):
                        last = pe.matmul(o[:, 0, :], hh[:, c, t * P:(t + 1) * P], wdT[:, c, :], start=(q == 0),
                                         stop=(q == len(terms) - 1))
                    last.then_inc(s_d, 1)

                def quantised(t, o):
                    for k in range(KT):
                        last = pe.matmul(o[:, 0, :], qiT[:, k, t * P:(t + 1) * P], rhs_q[:, k, :], start=(k == 0),
                                         stop=(k == KT - 1))
                    last.then_inc(s_a1, 1)

                pe.wait_ge(s_xn, QT)
                turn(RG[0], xn).then_inc(s_xt, 1)
                pe.wait_ge(s_xl, 1)
                queries(0, 0, RG[1])

                def body(h, plan, like, gu0, l2, l1, l0, ln):
                    n = UNITS * h

                    def bank(*use):
                        where, (before, d) = plan[use]
                        ls = kinds[like + d][0] if like + d >= 0 else (None, None, None, 0)
                        pe.wait_ge(*released(before, h + d, ls[0], ls[1]))
                        return RG[where]

                    for u in range(UNITS):
                        one, two, three = (l0 if u >= d else l1 for d in (1, 2, 3))
                        if l0 is not None:
                            scores(n + u, u, 64 * (h + 1))
                        if ("q", u) in plan:
                            if u == UNITS - 1:
                                pe.wait_ge(s_xl, h + 2)
                            queries((u + 1) % UNITS, l0 if u < UNITS - 1 else ln, bank("q", u))
                        if three is not None:
                            if u == 3 and l1 is not None:
                                pe.wait_ge(s_x1, h)
                            project(n + u - 3, (u - 3) % UNITS, three)
                        if l2 == 0 and u < 2:
                            gate_up(2 * u + 1, bank("gu", 2 * u + 1))
                        if ("turned_x", 0) in plan and u == 2:
                            pe.wait_ge(s_xn, QT * (h + 2))
                            turn(bank("turned_x", 0), xn).then_inc(s_xt, 1)
                        if two is not None:
                            weigh_values(n + u - 2, (u - 2) % UNITS, 16 * (h if u < 2 else h + 1))
                        if l2 == 0 and u == 3:
                            pe.wait_ge(s_hl, HC * (h - 1))
                            down(0, bank("down", 0))
                        if l2 == 1 and u == 1:
                            pe.wait_ge(s_qi, h - 1 - B)
                            turn(as_f16(bank("turned_q", 0)), q_i).then_inc(s_qt, 1)
                        if one is not None:
                            turn_probabilities(n + u - 1)
                        if l1 == 0 and u == 3:
                            pe.wait_ge(s_x2, QT * h)
                            turn(bank("turned_x2", 0), x2).then_inc(s_xt2, 1)
                        if l2 == 0 and u < 3:
                            c = (2, 4, 5)[u]
                            gate_up(c, bank("gu", c))
                        if l2 == 1 and u == 1:
                            pe.wait_ge(s_qe, h - 1 - B)
                            for t in range(QT):
                                quantised(t, bank("down", t))
                        if l2 == 0 and u == 3:
                            down(1, bank("down", 1))
                        if l1 == 0 and u == 3:
                            pe.wait_ge(s_x2l, h)
                            gate_up(0, bank("gu", 0))

                bodies(pe, body)

            @block.scalar
            def _(act):
                def high(dst, src):
                    return act.activation(dst, src, ACT.Copy)

                act.wait_ge(s_xt, 1)
                high(xT_h[:, :, :], RG[0]).then_inc(s_xh, 1)
                act.wait_ge(s_q, 1)
                high(qT_h[:, :, :], RG[1]).then_inc(s_qh, 1)

                def body(h, plan, like, gu0, l2, l1, l0, ln):
                    n = UNITS * h

                    def bank(*use):
                        return RG[plan[use][0]]

                    def tanh_gate(c, b):
                        act.wait_ge(s_g, HC * b + c + 1)
                        act.activation(th[:, c % 2, :], bank("gu", c)[:, 0, :], ACT.Tanh,
                                       scale=G_SCALE).then_inc(s_th, 1)

                    def high_hidden(c):
                        act.wait_ge(s_hf, HC * (h - 2) + c + 1)
                        high(hT_h[:, c, :], hf[:, c % 2, :]).then_inc(s_hh, 1)

                    def exponentials(n, t):
                        for b in range(HPU):
                            last = act.activation(ex[:, t, b, :], SC[:, t, b * NK:(b + 1) * NK], ACT.Exp,
                                                  bias=nmax[:, t, b:b + 1], accum_out=den[:, t, b:b + 1])
                        last.then_inc(s_e, 1)

                    for u in range(UNITS):
                        one, two = (l0 if u >= d else l1 for d in (1, 2))
                        if l0 is not None:
                            if not (isinstance(n, int) and n + u == 0):
                                act.wait_ge(s_p, n + u)
                            act.wait_ge(s_m, n + u + 1)
                            exponentials(n + u, 0)
                        if l2 == 0:
                            high_hidden((0, 2, 4, 5)[u])
                        if l2 == 1 and u == 1:
                            act.wait_ge(s_qb, h - 1 - B)
                            act.activation(q_i[:, :, :], q_b[:, :, :], ACT.Copy, bias=-MAGIC).then_inc(s_qi, 1)
                        if ("q", u) in plan:
                            act.wait_ge(s_q, n + u + 2)
                            high(qT_h[:, :, :], bank("q", u)).then_inc(s_qh, 1)
                        if l0 is not None:
                            exponentials(n + u, 1)
                        if l2 == 1 and u == 0:
                            act.wait_ge(s_li, h - 1 - B)
                            for t in range(QT):
                                act.activation(q_a[:, t, :], x2[:, t, :], ACT.Copy, scale=linv[:, t:t + 1],
                                               bias=MAGIC).then_inc(s_qa, 1)
                        if l2 == 0 and u < 2:
                            tanh_gate(2 * u + 1, h - 2)
                        if ("turned_x", 0) in plan and u == 2:
                            act.wait_ge(s_xt, h + 2)
                            high(xT_h[:, :, :], bank("turned_x", 0)).then_inc(s_xh, 1)
                        if two is not None:
                            act.wait_ge(s_pv, n + u - 1)
                            high(oT_h[:, :, :], OV).then_inc(s_oh, 1)
                        if l1 == 0 and u == 3:
                            act.wait_ge(s_xt2, h)
                            high(x2T_h[:, :, :], bank("turned_x2", 0)).then_inc(s_x2h, 1)
                        if l2 == 0 and u < 2:
                            high_hidden(2 * u + 1)
                        if one is not None:
                            for a in range(PPU):
                                act.wait_ge(s_t, 2 * (n + u - 1) + a + 1)
                                high(pT_h[:, 2 * a:2 * a + 2, :], PT[:, a]).then_inc(s_ph, 1)
                        if l2 == 0 and u < 3:
                            tanh_gate((2, 4, 5)[u], h - 2)
                        if l1 == 0 and u == 3:
                            tanh_gate(0, h - 1)

                bodies(act, body)

            @block.vector
            def _(dve):
                def low(dst, src, hi):
                    if hi.dtype == F32R:
                        hi = hi.bitcast(F32)
                    return dve.tensor_tensor(dst, src, hi, ALU.subtract)

                def stats(src, st, s_done):
                    for t in range(QT):
                        dve.bn_stats(st[:, t, :], src[:, t, :]).then_inc(s_done, 1)

                def aggregate(st, mv, s_done):
                    for t in range(QT):
                        dve.bn_aggr(mv[:, t, :], st[:, t, :]).then_inc(s_done, 1)

                def normalise(dst, src, mv, rs, s_rs_, s_done, g):
                    dve.wait_ge(s_rs_, g + 1)
                    for t in range(QT):
                        dve.tensor_scalar(dst[:, t, :], src[:, t, :], mv[:, t, 0:1], rs[:, t:t + 1],
                                          ALU.subtract, ALU.mult).then_inc(s_done, 1)

                dve.wait_ge(s_x, 16)
                stats(x_in, st1, s_st)
                dve.wait_ge(s_st, QT)
                aggregate(st1, mv1, s_mv)
                normalise(xn, x_in, mv1, rs1, s_rs, s_xn, 0)
                dve.wait_ge(s_xh, 1)
                low(xT_l[:, :, :], RG[0], xT_h[:, :, :]).then_inc(s_xl, 1)
                dve.wait_ge(s_qh, 1)
                low(qT_l[:, :, :], RG[1], qT_h[:, :, :]).then_inc(s_ql, 1)

                def body(h, plan, like, gu0, l2, l1, l0, ln):
                    n = UNITS * h

                    def bank(*use):
                        return RG[plan[use][0]]

                    def hidden(c):
                        k = HC * (h - 2) + c
                        o = RG[gu0] if c == 0 else bank("gu", c)
                        dve.wait_ge(s_th, k + 1)
                        dve.scalar_tensor_tensor(out=sg[:, c % 2, :], in0=th[:, c % 2, :], scalar=1.0,
                                                 in1=o[:, 0, :], op0=ALU.add, op1=ALU.mult).then_inc(s_sg, 1)
                        dve.wait_ge(s_sg, k + 1)
                        if c >= 2:
                            dve.wait_ge(s_hl, k - 1)
                        dve.tensor_tensor(hf[:, c % 2, :], o[:, 1, :], sg[:, c % 2, :], ALU.mult).then_inc(s_hf, 1)

                    def out_rows(t):
                        dve.wait_ge(s_d, QT * (h - 2) + t + 1)
                        dve.wait_ge(s_yx, h - 1)
                        dve.scalar_tensor_tensor(out=y[:, t, :], in0=bank("down", t)[:, 0, :], scalar=FFN_SCALE,
                                                 in1=y[:, t, :], op0=ALU.mult, op1=ALU.add).then_inc(s_yd, 1)

                    def descale(t):
                        dve.wait_ge(s_a1, QT * (h - 2 - B) + t + 1)
                        dve.scalar_tensor_tensor(out=ya[:, t, :], in0=bank("down", t)[:, 0, :],
                                                 scalar=lsc[:, t:t + 1], in1=rhs_sb[:, :], op0=ALU.mult,
                                                 op1=ALU.mult).then_inc(s_ya, 1)

                    for u in range(UNITS):
                        two = l0 if u >= 2 else l1
                        if l0 is not None:
                            dve.wait_ge(s_s, n + u + 1)
                            dve.tensor_reduce(nmax[:, :, :], SC.rearrange("p t (h k) -> p t h k", k=NK), AX_X,
                                              ALU.max, negate=True).then_inc(s_m, 1)
                        if l2 == 0:
                            hidden((0, 2, 4, 5)[u])
                        if l0 is not None and ln is not None and u == 2:
                            normalise(xn, x_in, mv1, rs1, s_rs, s_xn, h + 1)
                        if two is not None:
                            for a in range(PPU):
                                dve.wait_ge(s_ph, 2 * (n + u - 2) + a + 1)
                                low(pT_l[:, 2 * a:2 * a + 2, :], PT[:, a],
                                    pT_h[:, 2 * a:2 * a + 2, :]).then_inc(s_pl, 1)
                        if l0 is not None and ln is not None and u == 1:
                            dve.wait_ge(s_x, 16 * (h + 2))
                            stats(x_in, st1, s_st)
                            dve.wait_ge(s_st, QT * (h + 2))
                        if l2 == 1 and u == 0:
                            normalise(x2, x1, mv2, rs2, s_rs2, s_x2, h - 2)
                        if l1 == 1 and u == 3:
                            dve.wait_ge(s_x1, h)
                            stats(x1, st2, s_st2)
                            dve.wait_ge(s_st2, QT * h)
                        if l1 == 0 and u == 3:
                            normalise(x2, x1, mv2, rs2, s_rs2, s_x2, h - 1)
                        if ("q", u) in plan:
                            dve.wait_ge(s_qh, n + u + 2)
                            low(qT_l[:, :, :], bank("q", u), qT_h[:, :, :]).then_inc(s_ql, 1)
                        if l1 == 1 and u == 3:
                            aggregate(st2, mv2, s_mv2)
                        if l0 is not None and ln is not None and u == 1:
                            aggregate(st1, mv1, s_mv)
                        if l2 == 1 and u == 0:
                            g = h - 2 - B
                            dve.wait_ge(s_x2, QT * (h - 1))
                            dve.tensor_reduce(am[:, :], x2[:, :, :], AX_X, ALU.max,
                                              apply_absolute_value=True).then_inc(s_am, 1)
                            dve.wait_ge(s_am, g + 1)
                            dve.tensor_scalar(lsc[:, :], am[:, :], 1e-12, 1.0 / INT8_MAX, ALU.max,
                                              ALU.mult).then_inc(s_ls, 1)
                            dve.wait_ge(s_ls, g + 1)
                            dve.reciprocal(linv[:, :], lsc[:, :]).then_inc(s_li, 1)
                        if l0 is not None:
                            dve.wait_ge(s_e, QT * (n + u + 1))
                            dve.reciprocal(rden[:, :, :], den[:, :, :]).then_inc(s_r, 1)
                        if l2 == 0 and u < 2:
                            hidden(2 * u + 1)
                        if l2 == 1 and u == 1:
                            dve.wait_ge(s_qt, h - 1 - B)
                            dve.tensor_copy(qiT[:, :, :], as_f16(bank("turned_q", 0))).then_inc(s_qe, 1)
                        if l1 is not None and u == 2:
                            dve.wait_ge(s_oa, h)
                            dve.wait_ge(s_xb, h)
                            if l2 == 0:
                                dve.wait_ge(s_yx, h - 1)
                            elif l2 == 1:
                                dve.wait_ge(s_yq, h - 1 - B)
                            dve.tensor_tensor(x1[:, :, :], OA, x_res[:, :, :], ALU.add).then_inc(s_x1, 1)
                        if l2 == 0 and u == 3:
                            out_rows(0)
                        if ("turned_x", 0) in plan and u == 2:
                            dve.wait_ge(s_xh, h + 2)
                            low(xT_l[:, :, :], bank("turned_x", 0), xT_h[:, :, :]).then_inc(s_xl, 1)
                        if l1 == 0 and u == 2:
                            dve.wait_ge(s_x1, h)
                            stats(x1, st2, s_st2)
                            dve.wait_ge(s_st2, QT * h)
                        if l2 == 1 and u == 0:
                            dve.wait_ge(s_qa, QT * (h - 1 - B))
                            dve.tensor_scalar(q_b[:, :, :], q_a[:, :, :], MAGIC - INT8_MAX, MAGIC + INT8_MAX,
                                              ALU.max, ALU.min).then_inc(s_qb, 1)
                        if two is not None:
                            dve.wait_ge(s_oh, n + u - 1)
                            low(oT_l[:, :, :], OV, oT_h[:, :, :]).then_inc(s_ol, 1)
                        if l1 == 0 and u == 2:
                            aggregate(st2, mv2, s_mv2)
                        if l2 == 1 and u == 1:
                            for t in range(QT):
                                descale(t)
                        if l1 == 0 and u == 3:
                            dve.wait_ge(s_x2h, h)
                            low(x2T_l[:, :, :], bank("turned_x2", 0), x2T_h[:, :, :]).then_inc(s_x2l, 1)
                        if l2 == 0 and u == 3:
                            out_rows(1)

                bodies(dve, body)

            @block.gpsimd
            def _(pool):
                for u in range(UNITS):
                    pool.memset(kb[u][:, :, :, :], 0.0).then_inc(s_kz, 1)

                def inverse_deviation(mv, ve, rs, s_mv_, s_ve_, s_rs_, g):
                    pool.wait_ge(s_mv_, QT * (g + 1))
                    pool.tensor_tensor(ve[:, :], mv[:, :, 1], eps[:, :], ALU.add).then_inc(s_ve_, 1)
                    pool.wait_ge(s_ve_, g + 1)
                    pool.tensor_tensor(rs[:, :], ve[:, :], half_neg[:, :], ALU.pow).then_inc(s_rs_, 1)

                inverse_deviation(mv1, ve1, rs1, s_mv, s_ve, s_rs, 0)

                def body(h, plan, like, gu0, l2, l1, l0, ln):
                    n = UNITS * h

                    def low_hidden(c):
                        pool.wait_ge(s_hh, HC * (h - 2) + c + 1)
                        pool.tensor_tensor(hT_l[:, c, :], hf[:, c % 2, :], hT_h[:, c, :].bitcast(F32),
                                           ALU.subtract).then_inc(s_hl, 1)

                    for u in range(UNITS):
                        if l2 == 0:
                            low_hidden((0, 2, 4, 5)[u])
                        if l2 == 1 and u == 2:
                            pool.wait_ge(s_y, 16 * (h - 1))
                            pool.wait_ge(s_ya, QT * (h - 1 - B))
                            pool.tensor_tensor(y[:, :, :], ya[:, :, :], x1[:, :, :], ALU.add).then_inc(s_yq, 1)
                        if l1 is not None and u == 3:
                            inverse_deviation(mv2, ve2, rs2, s_mv2, s_ve2, s_rs2, h - 1)
                        if l0 is not None:
                            pool.wait_ge(s_r, n + u + 1)
                            if not (isinstance(n, int) and n + u == 0):
                                pool.wait_ge(s_t, 2 * (n + u))
                            r = rden[:, :, :].unsqueeze(3).to_broadcast([P, QT, HPU, NK])
                            pool.tensor_tensor(pr[:, :, :, :], ex[:, :, :, :], r, ALU.mult).then_inc(s_p, 1)
                        if u == 1 and l0 is not None and ln is not None:
                            inverse_deviation(mv1, ve1, rs1, s_mv, s_ve, s_rs, h + 1)
                        if u == 0 and l1 is not None:
                            pool.wait_ge(s_xr, 16 * h)
                            bias = bo_b[l1][:, :].unsqueeze(1).to_broadcast([P, QT, D])
                            pool.tensor_tensor(x_res[:, :, :], x_res[:, :, :], bias, ALU.add).then_inc(s_xb, 1)
                        if l2 == 0 and u == 1:
                            pool.wait_ge(s_y, 16 * (h - 1))
                        if l2 == 0 and u < 2:
                            low_hidden(2 * u + 1)
                        if l2 == 0 and u == 1:
                            pool.tensor_copy(y[:, :, :], x1[:, :, :]).then_inc(s_yx, 1)

                bodies(pool, body)


_INS = ['x', 'ctx_768', 'L0_xattn_Wq', 'L0_xattn_Wk', 'L0_xattn_Wv', 'L0_xattn_Wo', 'L0_xattn_bo',
        'L0_ffn_w_gate', 'L0_ffn_w_up', 'L0_ffn_w_down', 'L1_xattn_Wq', 'L1_xattn_Wk', 'L1_xattn_Wv',
        'L1_xattn_Wo', 'L1_xattn_bo', 'L1_ffn_rhs']
_OUTS = [((32, 256, 256), 'float32')]


def kernel(**inputs):
    import numpy as _np
    import concourse.bacc as _bacc
    from concourse import mybir as _mybir
    from concourse.bass_utils import run_bass_kernel_spmd as _run

    nc = _bacc.Bacc("TRN2", target_bir_lowering=False, num_devices=1)
    arrays, args = {}, []
    for name in _INS:
        a = _np.ascontiguousarray(inputs[name])
        arrays[f"in_{name}_dram"] = a
        args.append(nc.dram_tensor(f"in_{name}_dram", a.shape, _mybir.dt.from_np(a.dtype), kind="ExternalInput").ap())
    for i, (shape, dtype) in enumerate(_OUTS):
        dt = _mybir.dt.from_np(_np.dtype(dtype))
        args.append(nc.dram_tensor(f"out_{i}_dram", shape, dt, kind="ExternalOutput").ap())
    xattn_ffn_kernel(nc, *args)
    r = _run(nc, [arrays], core_ids=[0])
    return r.results[0]["out_0_dram"]
```

```python
from contextlib import ExitStack

import numpy as np
import concourse.bass as bass
from concourse import mybir

ALU = mybir.AluOpType
ACT = mybir.ActivationFunctionType
F32 = mybir.dt.float32
F32R = mybir.dt.float32r
F16 = mybir.dt.float16
I32 = mybir.dt.int32
AX_X = mybir.AxisListType.X

P = 128
HEADS, DH = 16, 64
UNITS = 4
HPU = HEADS // UNITS
PPU = HPU // 2
EPS = 1e-5
INT8_MAX = 127.0
MAGIC = 1.5 * 2.0 ** 23


def xattn_ffn_kernel(nc, x, ctx, wq0, wk0, wv0, wo0, bo0, w_gate, w_up, w_down,
                     wq1, wk1, wv1, wo1, bo1, rhs, out):
    B, NQ, D = x.shape
    NK, DC = ctx.shape[1], ctx.shape[2]
    INNER = HEADS * DH
    HID = w_gate.shape[0]
    QT = NQ // P
    KT = D // P
    MT = INNER // P
    HC = HID // P
    DCR = DC - P
    TOK = B * NK
    GRP = 352
    NG = TOK // GRP
    SUB = [(0, P), (P, P), (2 * P, GRP - 2 * P)]
    assert NG * GRP == TOK and DCR == 64 and KT == 2 and QT == 2 and HC == 6
    NB = 2 * B
    G_SCALE = 0.5 / INT8_MAX
    FFN_SCALE = 0.5 / INT8_MAX ** 3

    stack = ExitStack()
    with stack:
        def sb(name, shape, dt, where=stack):
            return where.enter_context(nc.sbuf_tensor(name, shape, dt))

        def sem(name):
            return stack.enter_context(nc.semaphore(name))

        keys_d = [nc.dram_tensor(f"keys_{l}", (2, MT, P, TOK), F16).ap() for l in range(2)]
        vals_d = [nc.dram_tensor(f"vals_{l}", (2, TOK, INNER), F16).ap() for l in range(2)]
        mid_d = nc.dram_tensor("mid_x", (B, NQ, D), F32).ap()

        ident = sb("ident", [P, P], F32)
        ident16 = sb("ident16", [P, P], F16)
        half_neg = sb("half_neg", [P, QT], F32)
        eps = sb("eps", [P, QT], F32)
        wq_h = [sb(f"wq_h{l}", [P, KT, INNER], F32R) for l in range(2)]
        wq_l = [sb(f"wq_l{l}", [P, KT, INNER], F32R) for l in range(2)]
        wo_h = [sb(f"wo_h{l}", [P, MT, D], F32R) for l in range(2)]
        wo_l = [sb(f"wo_l{l}", [P, MT, D], F32R) for l in range(2)]
        bo_b = [sb(f"bo_b{l}", [P, D], F32) for l in range(2)]
        wgT = sb("wgT", [P, KT, HID], F32R)
        wuT = sb("wuT", [P, KT, HID], F32R)
        wdT = sb("wdT", [P, HC, D], F32R)
        rhs_q = sb("rhs_q", [P, KT, D], F16)
        rhs_sb = sb("rhs_sb", [P, D], F32)
        x_pair = sb("x_pair", [P, 2, QT * D], F32)
        x_in, xn = (x_pair[:, i, :].rearrange("p (t d) -> p t d", d=D) for i in range(2))
        st1 = sb("st1", [P, QT, 6], F32)
        mv1 = sb("mv1", [P, QT, 2], F32)
        ve1 = sb("ve1", [P, QT], F32)
        rs1 = sb("rs1", [P, QT], F32)

        psum = stack.enter_context(nc.psum_tensor("psum", [P, 8, 512], F32))

        early = ExitStack()
        raw = sb("raw", [P, 2, INNER], F32, early)
        raw_f2 = sb("raw_f", [P, 2 * HID], F32, early)
        raw_f = [raw_f2[:, i * HID:(i + 1) * HID] for i in range(2)]
        r_amax = sb("r_amax", [P, KT], F32, early)
        r_scale = sb("r_scale", [P, KT], F32, early)
        r_inv = sb("r_inv", [P, KT], F32, early)
        r_q, r_q2 = x_in, xn
        r_sp = x_pair[:, 1, 0:P]
        kf_h = [[sb(f"w{k}{i}_h{l}", [P, INNER], F32R, early) for l in range(2)] for k in "kv" for i in range(2)]
        kf_l = [[sb(f"w{k}{i}_l{l}", [P, INNER], F32R, early) for l in range(2)] for k in "kv" for i in range(2)]
        cx = sb("cx", [P, 4, 2 * P], F32, early)
        c0h = [sb(f"c0h{i}", [P, GRP], F32R, early) for i in range(2)]
        c0l = [sb(f"c0l{i}", [P, GRP], F32R, early) for i in range(2)]
        c1 = [sb(f"c1{i}", [P, GRP], F32R, early) for i in range(2)]
        c1t = sb("c1t", [P, GRP], F32R, early)
        ks = sb("ks", [P, 2, MT, GRP], F16, early)
        vs = sb("vs", [P, 2, 3, INNER], F16, early)

        s_z = sem("s_z")
        s_k = [sem(f"s_k{j}") for j in range(8)]
        s_kh = sem("s_kh")
        s_kl = sem("s_kl")
        s_kp = sem("s_kp")
        s_ri = [sem("s_ri0"), sem("s_ri1")]
        s_rr = sem("s_rr")
        s_ro = [sem(f"s_ro{i}") for i in range(3)]
        s_int = sem("s_int")
        s_wt = sem("s_wt")
        s_wte = sem("s_wte")
        s_wh = sem("s_wh")
        s_wl = sem("s_wl")
        s_wp = sem("s_wp")
        s_bo = sem("s_bo")
        s_rq = sem("s_rq")
        s_rt = sem("s_rt")
        s_x = sem("s_x")
        s_st, s_mv, s_ve, s_rs, s_xn = (sem(f"s_{a}") for a in ("st", "mv", "ve", "rs", "xn"))

        kv_items = []
        for l, (wk, wv) in enumerate(((wk0, wv0), (wk1, wv1))):
            for k, w in ((0, wk), (2, wv)):
                kv_items.append(([(w[0:P, :], 0, P)], kf_h[k][l][:, :], kf_l[k][l][:, :], P))
                kv_items.append(([(w[P:DC, :], 0, DCR), (w[P:DC, :], DCR, DCR)],
                                 kf_h[k + 1][l][:, :], kf_l[k + 1][l][0:DCR, :], DCR))
        kv_raw = 2 * [raw[:, 0, :], raw[:, 1, :], raw_f2[:, 0:INNER], x_pair[:, :, :].rearrange("p i c -> p (i c)")]
        qo_items = []
        for l, (wq, wo) in enumerate(((wq0, wo0), (wq1, wo1))):
            for k in range(2):
                qo_items.append((wq[k * P:(k + 1) * P, :], wq_h[l][:, k, :], wq_l[l][:, k, :], DH ** -0.5))
                src = wo[k * 4 * P:(k + 1) * 4 * P, :].rearrange("(t p) d -> p t d", p=P)
                qo_items.append((src, wo_h[l][:, 4 * k:4 * k + 4, :].rearrange("p t d -> p (t d)"),
                                 wo_l[l][:, 4 * k:4 * k + 4, :].rearrange("p t d -> p (t d)"), 1.0))
        turned = []
        for w, wT in ((w_gate, wgT), (w_up, wuT)):
            for a in range(2):
                src = w[a * 3 * P:(a + 1) * 3 * P, :].rearrange("(t p) d -> p t d", p=P)
                blocks = [(t * D + k * P, k, t) for k in range(KT) for t in range(3)]
                turned.append((src, blocks, [wT[:, k, a * 3 * P:(a + 1) * 3 * P] for k in range(KT)]))
        for a in range(KT):
            src = w_down[a * P:(a + 1) * P, :]
            blocks = [(c * P, c // 3, c % 3) for c in range(HC)]
            turned.append((src, blocks, [wdT[:, 3 * k:3 * k + 3, a * P:(a + 1) * P] for k in range(2)]))
        qo_items, late_items = qo_items[:4], qo_items[4:]
        NQO, NT = len(qo_items), len(turned)
        cx_all = cx[:, :, :].rearrange("p t d -> p (t d)")
        rhs_raw = cx_all[:, 0:KT * D]
        qo_raw = [cx_all, raw[:, 0, :], raw[:, 1, :]]

        def qo_landed(eng, k):
            eng.wait_ge(s_ro[k % 3], 16 * (k // 3 + 1))

        s_cx = sem("s_cx")
        s_ct = sem("s_ct")
        s_ch = sem("s_ch")
        s_cl = sem("s_cl")
        s_kv = sem("s_kv")
        s_kvh = sem("s_kvh")
        s_kvf = sem("s_kvf")
        SK, SV = 16 * 2, 16 * 2 * 3
        s_sk = sem("s_sk")
        s_sv = sem("s_sv")
        HALVES = INNER // 512
        KVL = MT + 3 * HALVES
        KVT = 2 * KVL
        RING = 4
        assert KVT % RING == 0

        def kv_tiles():
            for l in range(2):
                for m in range(MT):
                    yield l, "k", m, 0
                for t in range(3):
                    for hf in range(HALVES):
                        yield l, "v", t, hf

        def kv_place(kind, a, b):
            if kind == "k":
                return P, GRP, lambda part: ks[:, part, a, :]
            rows = SUB[a][1]
            return rows, 512, lambda part: vs[0:rows, part, a, b * 512:(b + 1) * 512]

        def staging_free(eng, i, l, kind, a, b):
            if kind == "k" and a == 0:
                eng.wait_ge(s_sk, SK * (2 * i + l + 1))
            if kind == "v" and a == 0 and b == 0:
                eng.wait_ge(s_sv, SV * (2 * i + l + 1))

        ctx_t = ctx.rearrange("b k c -> (b k) c")

        assert NG % 2 == 1
        CONVERT_AT = [1, 6, 8, 10, 12, 14]
        TURN_INT_AT = [3, 8, 10, 12, 14, 16]
        INT_AT = [4, 9, 11, 13, 15, 17]
        QO_AT = [10, 16, 18, 20]
        Q_LOW_AT = [11, 19]
        TURN_AT, SPLIT_AT = 14, 16

        def groups(eng, group):
            with eng.Fori(0, NG - 1, 2) as i:
                group(i, 0)
                group(i + 1, 1)

        with nc.Block() as block:
            @block.sync
            def _(sp):
                def load_group(i):
                    for (t0, n), t in zip(SUB, range(3)):
                        rows = ctx_t[bass.ds(i * GRP + t0, n), :]
                        sp.dma_start(cx[0:n, t, 0:DC], rows).then_inc(s_cx, 16)
                        sp.dma_start(cx[0:n, t, DC:2 * P], rows[:, P:DC]).then_inc(s_cx, 16)

                def load_item(j):
                    for src, p0, n in kv_items[j][0]:
                        sp.dma_start(kv_raw[j][p0:p0 + n, :], src).then_inc(s_k[j], 16)

                load_item(0)
                load_item(1)
                load_group(0)
                for j in range(2, 4):
                    load_item(j)
                sp.sem_inc(s_sk, SK)
                sp.sem_inc(s_sv, SV)
                for j in range(4, 8):
                    sp.wait_ge(s_kl, j - 3)
                    load_item(j)
                    if j == 5:
                        sp.wait_ge(s_ct, 2)
                        load_group(1)
                for l, bo in enumerate((bo0, bo1)):
                    src = bo.rearrange("(o d) -> o d", o=1).to_broadcast([P, D])
                    sp.dma_start(bo_b[l][:, :], src).then_inc(s_bo, 16)

                def stores(i):
                    for l in range(2):
                        sp.wait_ge(s_kvf, RING + i * KVT + l * KVL + MT)
                        for part in range(2):
                            sp.dma_start(keys_d[l][part].rearrange("m p t -> p m t")[:, :, bass.ds(i * GRP, GRP)],
                                         ks[:, part, :, :]).then_inc(s_sk, 16)
                        sp.wait_ge(s_kvf, RING + i * KVT + (l + 1) * KVL)
                        for (t0, n), t in zip(SUB, range(3)):
                            for part in range(2):
                                sp.dma_start(vals_d[l][part, bass.ds(i * GRP + t0, n), :],
                                             vs[0:n, part, t, :]).then_inc(s_sv, 16)

                def group(i):
                    stores(i)
                    sp.wait_ge(s_ct, 2 * i + 4)
                    load_group(i + 2)

                with sp.Fori(0, NG - 2) as i:
                    group(i)
                stores(NG - 2)
                sp.wait_ge(s_rt, 4)
                sp.dma_start(x_in, x[0].rearrange("(t p) d -> p t d", p=P)).then_inc(s_x, 16)
                stores(NG - 1)
                sp.wait_ge(s_sk, SK * (2 * NG + 1))
                sp.wait_ge(s_sv, SV * (2 * NG + 1))
                sp.wait_ge(s_bo, 32)

            @block.gpsimd
            def _(pool):
                for t, value in ((ident, 0.0), (ident16, 0.0), (half_neg, -0.5), (eps, EPS)):
                    pool.memset(t[:, :], value).then_inc(s_z, 1)
                pool.wait_ge(s_z, 4)
                for t in (ident, ident16):
                    pool.affine_select(out=t[:, :], in_=t[:, :], compare_op=ALU.not_equal, fill=1.0, base=0,
                                       pattern=[[-1, P]], channel_multiplier=1).then_inc(s_z, 1)
                done = 0
                for j in range(4, 8):
                    _, hi, lo, rows = kv_items[j]
                    if j < 6:
                        pool.wait_ge(s_kh, j + 1)
                    else:
                        pool.wait_ge(s_k[j], 16 * len(kv_items[j][0]))
                        pool.tensor_copy(hi, kv_raw[j]).then_inc(s_kp, 1)
                        done += 1
                        pool.wait_ge(s_kp, done)
                    pool.tensor_tensor(lo, kv_raw[j][0:rows, :], hi[0:rows, :].bitcast(F32),
                                       ALU.subtract).then_inc(s_kp, 1)
                    done += 1

                def load_ints(j):
                    pool.wait_ge(*((s_kp, j + 1) if j < 2 else (s_int, j - 1)))
                    d, src = raw[:, j % 2, 0:HID].bitcast(I32), turned[j][0]
                    if len(src.shape) == 3:
                        d = d.rearrange("p (t d) -> p t d", d=D)
                    pool.dma_start(d, src).then_inc(s_ri[j % 2], 16)

                def load_qo(k):
                    if k == 0:
                        pool.wait_ge(s_rt, 1)
                    elif k < 3:
                        pool.wait_ge(s_int, NT - 2 + k)
                    else:
                        g = k - 3
                        pool.wait_ge(*((s_wl, g // 2 + 1) if g % 2 == 0 else (s_wp, g // 2 + 1)))
                    d, src = qo_raw[k % 3], qo_items[k][0]
                    if len(src.shape) == 3:
                        d = d.rearrange("p (t d) -> p t d", d=D)
                    pool.dma_start(d, src).then_inc(s_ro[k % 3], 16)

                load_ints(0)
                load_ints(1)
                pool.wait_ge(s_ct, 2 * NG)
                pool.dma_start(rhs_raw.rearrange("p (t d) -> p t d", d=D),
                               rhs.rearrange("(t p) d -> p t d", p=P)).then_inc(s_rr, 16)
                load_ints(2)
                load_qo(0)
                for j in range(3, NT):
                    load_ints(j)
                for k in (1, 3, 2):
                    load_qo(k)
                for k in (1, 3):
                    _, hi, lo, scale = qo_items[k]
                    pool.wait_ge(s_wh, k + 1)
                    pool.tensor_tensor(lo, qo_raw[k % 3], hi.bitcast(F32), ALU.subtract).then_inc(s_wp, 1)
                pool.wait_ge(s_mv, QT)
                pool.tensor_tensor(ve1[:, :], mv1[:, :, 1], eps[:, :], ALU.add).then_inc(s_ve, 1)
                pool.wait_ge(s_ve, 1)
                pool.tensor_tensor(rs1[:, :], ve1[:, :], half_neg[:, :], ALU.pow).then_inc(s_rs, 1)

            @block.scalar
            def _(act):
                def kv_high(j):
                    act.wait_ge(s_k[j], 16 * len(kv_items[j][0]))
                    act.activation(kv_items[j][1], kv_raw[j], ACT.Copy).then_inc(s_kh, 1)

                def split_group(i, par):
                    act.wait_ge(s_ct, 2 * i + 1)
                    act.activation(c0h[par][:, :], psum[:, 0, 0:GRP], ACT.Copy).then_inc(s_ch, 1)
                    act.wait_ge(s_ct, 2 * i + 2)
                    act.wait_ge(s_cl, 2 * i)
                    act.activation(c1t[DCR:P, :], psum[DCR:P, 1, 0:GRP], ACT.Copy).then_inc(s_ch, 1)
                    act.activation(c1[par][0:DCR, :], psum[0:DCR, 1, 0:GRP], ACT.Copy).then_inc(s_ch, 1)

                def high_tile(i, j, l, kind, a, b):
                    rows, cols, place = kv_place(kind, a, b)
                    staging_free(act, i, l, kind, a, b)
                    act.wait_ge(s_kv, i * KVT + j + 1)
                    act.activation(place(0), psum[0:rows, 2 + j % RING, 0:cols], ACT.Copy).then_inc(s_kvh, 1)

                kv_high(0)
                kv_high(1)
                act.wait_ge(s_ct, 1)
                act.activation(c0h[0][:, :], psum[:, 0, 0:GRP], ACT.Copy).then_inc(s_ch, 1)
                act.wait_ge(s_ct, 2)
                act.activation(c1t[DCR:P, :], psum[DCR:P, 1, 0:GRP], ACT.Copy).then_inc(s_ch, 1)
                act.activation(c1[0][0:DCR, :], psum[0:DCR, 1, 0:GRP], ACT.Copy).then_inc(s_ch, 1)
                for j in range(2, 6):
                    kv_high(j)

                def group(i, par):
                    for j, tile in enumerate(kv_tiles()):
                        high_tile(i, j, *tile)
                        if j == SPLIT_AT:
                            split_group(i + 1, 1 - par)

                groups(act, group)

                def copy_turned(j):
                    act.wait_ge(s_wt, j + 1)
                    for k, o in enumerate(turned[j][2]):
                        src = psum[:, 6 + k, 0:3 * P]
                        if len(o.shape) == 3:
                            src = src.rearrange("p (t d) -> p t d", d=P)
                        act.activation(o, src, ACT.Copy).then_inc(s_wte, 1)

                def qo_high(k):
                    _, hi, lo, scale = qo_items[k]
                    qo_landed(act, k)
                    act.activation(hi, qo_raw[k % 3], ACT.Copy, scale=scale).then_inc(s_wh, 1)

                for j, tile in enumerate(kv_tiles()):
                    high_tile(NG - 1, j, *tile)
                    if j in INT_AT:
                        copy_turned(INT_AT.index(j))
                    if j in QO_AT:
                        qo_high(QO_AT.index(j))
                for k in range(len(QO_AT), NQO):
                    qo_high(k)

            @block.vector
            def _(dve):
                def kv_low(j):
                    _, hi, lo, rows = kv_items[j]
                    dve.wait_ge(s_kh, j + 1)
                    dve.tensor_tensor(lo, kv_raw[j][0:rows, :], hi[0:rows, :].bitcast(F32), ALU.subtract).then_inc(s_kl, 1)

                def split_group(i, par):
                    dve.wait_ge(s_ch, 3 * i + 1)
                    dve.tensor_tensor(c0l[par][:, :], psum[:, 0, 0:GRP], c0h[par][:, :].bitcast(F32),
                                      ALU.subtract).then_inc(s_cl, 1)
                    dve.wait_ge(s_ch, 3 * i + 3)
                    dve.tensor_tensor(c1[par][DCR:P, :], psum[DCR:P, 1, 0:GRP], c1t[DCR:P, :].bitcast(F32),
                                      ALU.subtract).then_inc(s_cl, 1)

                def low_tile(i, j, l, kind, a, b):
                    rows, cols, place = kv_place(kind, a, b)
                    dve.wait_ge(s_kvh, i * KVT + j + 1)
                    dve.tensor_tensor(place(1), psum[0:rows, 2 + j % RING, 0:cols], place(0),
                                      ALU.subtract).then_inc(s_kvf, 1)

                kv_low(0)
                kv_low(1)
                split_group(0, 0)
                kv_low(2)
                kv_low(3)

                def group(i, par):
                    for j, tile in enumerate(kv_tiles()):
                        low_tile(i, j, *tile)
                        if j == SPLIT_AT:
                            split_group(i + 1, 1 - par)

                groups(dve, group)

                def convert(j):
                    dve.wait_ge(s_ri[j % 2], 16 * (j // 2 + 1))
                    if j < 2:
                        dve.wait_ge(s_kp, 4)
                    else:
                        dve.wait_ge(s_wt, j - 1)
                    dve.tensor_copy(raw_f[j % 2], raw[:, j % 2, 0:HID].bitcast(I32)).then_inc(s_int, 1)

                def q_low(k):
                    _, hi, lo, scale = qo_items[k]
                    dve.wait_ge(s_wh, k + 1)
                    dve.scalar_tensor_tensor(out=lo, in0=qo_raw[k % 3], scalar=scale,
                                             in1=hi.bitcast(F32), op0=ALU.mult, op1=ALU.subtract).then_inc(s_wl, 1)

                def scales_of_rhs():
                    dve.wait_ge(s_rt, 1)
                    rt = psum[:, 0, :].rearrange("p (t d) -> p t d", d=D)
                    dve.tensor_reduce(r_amax[:, :], rt, AX_X, ALU.max, apply_absolute_value=True).then_inc(s_rq, 1)
                    dve.wait_ge(s_rq, 1)
                    dve.tensor_scalar(r_scale[:, :], r_amax[:, :], 1e-12, 1.0 / INT8_MAX, ALU.max,
                                      ALU.mult).then_inc(s_rq, 1)
                    dve.wait_ge(s_rq, 2)
                    dve.reciprocal(r_inv[:, :], r_scale[:, :]).then_inc(s_rq, 1)
                    dve.wait_ge(s_rq, 3)
                    dve.wait_ge(s_kp, 6)
                    for t in range(KT):
                        dve.tensor_scalar(r_q[:, t, :], rt[:, t, :], r_inv[:, t:t + 1], INT8_MAX, ALU.mult,
                                          ALU.min).then_inc(s_rq, 1)

                def round_rhs():
                    dve.wait_ge(s_rq, 5)
                    dve.tensor_scalar(r_q2, r_q, -INT8_MAX, MAGIC, ALU.max, ALU.add).then_inc(s_rq, 1)
                    dve.wait_ge(s_rq, 6)
                    dve.tensor_scalar(r_q, r_q2, MAGIC, None, ALU.subtract).then_inc(s_rq, 1)

                def spread_scale(t):
                    if t == 0:
                        dve.wait_ge(s_rq, 7)
                    else:
                        dve.wait_ge(s_rt, 3)
                    dve.tensor_scalar(r_sp, ident[:, :], 0.0, r_scale[:, t:t + 1], ALU.mult, ALU.add).then_inc(s_rq, 1)

                def place_rhs():
                    dve.wait_ge(s_rt, 2)
                    dve.tensor_copy(rhs_q[:, :, :], psum[:, 1, :].rearrange("p (t d) -> p t d", d=D)).then_inc(s_rq, 1)

                for j, tile in enumerate(kv_tiles()):
                    if j in CONVERT_AT:
                        convert(CONVERT_AT.index(j))
                    low_tile(NG - 1, j, *tile)
                    if j in Q_LOW_AT:
                        q_low(2 * Q_LOW_AT.index(j))
                    if j == 2:
                        scales_of_rhs()
                    if j == 4:
                        round_rhs()
                    if j == 5:
                        spread_scale(0)
                    if j == 9:
                        spread_scale(1)
                        place_rhs()
                    if j == 13:
                        dve.wait_ge(s_rt, 4)
                        dve.tensor_copy(rhs_sb[:, :], psum[:, 0, 0:D]).then_inc(s_rq, 1)
                for k in range(len(Q_LOW_AT), NQO // 2):
                    q_low(2 * k)
                dve.wait_ge(s_x, 16)
                for t in range(QT):
                    dve.bn_stats(st1[:, t, :], x_in[:, t, :]).then_inc(s_st, 1)
                dve.wait_ge(s_st, QT)
                for t in range(QT):
                    dve.bn_aggr(mv1[:, t, :], st1[:, t, :]).then_inc(s_mv, 1)
                dve.wait_ge(s_rs, 1)
                for t in range(QT):
                    dve.tensor_scalar(xn[:, t, :], x_in[:, t, :], mv1[:, t, 0:1], rs1[:, t:t + 1],
                                      ALU.subtract, ALU.mult).then_inc(s_xn, 1)

            @block.tensor
            def _(pe):
                def turn_group(i):
                    pe.wait_ge(s_cx, 96 * i + 96)
                    for k in range(2):
                        for (t0, n), t in zip(SUB, range(3)):
                            last = pe.transpose(psum[:, k, t0:t0 + n], cx[0:n, t, k * P:(k + 1) * P],
                                                ident[0:n, 0:n])
                        last.then_inc(s_ct, 1)

                def tile_product(i, par, j, l, kind, a, b):
                    if l == 0:
                        pe.wait_ge(s_kl, 2 if kind == "k" else 4)
                    else:
                        pe.wait_ge(s_kp, 2 if kind == "k" else 6)
                    rows, cols, _ = kv_place(kind, a, b)
                    pe.wait_ge(s_kvf, i * KVT + j + 1)
                    o = psum[0:rows, 2 + j % RING, 0:cols]
                    h0, l0, h1 = c0h[par], c0l[par], c1[par]
                    if kind == "k":
                        w = slice(a * P, (a + 1) * P)
                        terms = [(kf_h[0][l][:, w], h0[:, :]), (kf_h[0][l][:, w], l0[:, :]),
                                 (kf_l[0][l][:, w], h0[:, :]), (kf_h[1][l][:, w], h1[:, :]),
                                 (kf_l[1][l][0:DCR, w], h1[0:DCR, :])]
                    else:
                        w = slice(b * 512, (b + 1) * 512)
                        ts = slice(SUB[a][0], SUB[a][0] + rows)
                        terms = [(h0[:, ts], kf_h[2][l][:, w]), (l0[:, ts], kf_h[2][l][:, w]),
                                 (h0[:, ts], kf_l[2][l][:, w]), (h1[:, ts], kf_h[3][l][:, w]),
                                 (h1[0:DCR, ts], kf_l[3][l][0:DCR, w])]
                    for q, (lhsT, r) in enumerate(terms):
                        last = pe.matmul(o, lhsT, r, start=(q == 0), stop=(q == len(terms) - 1))
                    last.then_inc(s_kv, 1)

                pe.sem_inc(s_kvf, RING)
                pe.wait_ge(s_z, 6)
                turn_group(0)

                def group(i, par):
                    pe.wait_ge(s_cl, 2 * i + 2)
                    for j, tile in enumerate(kv_tiles()):
                        tile_product(i, par, j, *tile)
                        if j == TURN_AT:
                            turn_group(i + 1)

                groups(pe, group)

                def turn_ints(j):
                    pe.wait_ge(s_int, j + 1)
                    if j >= 1:
                        pe.wait_ge(s_wte, 2 * j)
                    for c, k, t in turned[j][1]:
                        last = pe.transpose(psum[:, 6 + k, t * P:(t + 1) * P],
                                            raw_f[j % 2][:, c:c + P], ident[:, :])
                    last.then_inc(s_wt, 1)

                def turn_rhs():
                    pe.wait_ge(s_rr, 16)
                    pe.wait_ge(s_cl, 2 * NG)
                    for t in range(KT):
                        for k in range(KT):
                            last = pe.transpose(psum[:, 0, t * D + k * P:t * D + (k + 1) * P],
                                                rhs_raw[:, k * D + t * P:k * D + (t + 1) * P], ident[:, :])
                    last.then_inc(s_rt, 1)

                def turn_back():
                    pe.wait_ge(s_rq, 7)
                    for k in range(KT):
                        for t in range(KT):
                            last = pe.transpose(psum[:, 1, k * D + t * P:k * D + (t + 1) * P],
                                                r_q[:, t, k * P:(k + 1) * P], ident[:, :])
                    last.then_inc(s_rt, 1)

                def turn_scales(t, steps):
                    pe.wait_ge(s_rq, steps)
                    pe.transpose(psum[:, 0, t * P:(t + 1) * P], r_sp, ident[:, :]).then_inc(s_rt, 1)

                pe.wait_ge(s_cl, 2 * NG)
                for j, tile in enumerate(kv_tiles()):
                    tile_product(NG - 1, (NG - 1) % 2, j, *tile)
                    if j in TURN_INT_AT:
                        turn_ints(TURN_INT_AT.index(j))
                    if j == 0:
                        turn_rhs()
                    if j == 8:
                        turn_back()
                        turn_scales(0, 8)
                    if j == 11:
                        turn_scales(1, 9)

        early.close()

        late_raw = sb("late_raw", [P, len(late_items), INNER], F32)
        x_res = sb("x_res", [P, QT, D], F32)
        xT_h = sb("xT_h", [P, KT, NQ], F32R)
        xT_l = sb("xT_l", [P, KT, NQ], F32R)
        kb = [sb(f"kb{u}", [P, 2, PPU, 2 * NK], F16) for u in range(UNITS)]
        vb = [sb(f"vb{u}", [NK, 2, HPU * DH], F16) for u in range(UNITS)]
        qT_h = sb("qT_h", [P, PPU, NQ], F16)
        qT_l = sb("qT_l", [P, PPU, NQ], F16)
        nmax = sb("nmax", [P, QT, HPU], F32)
        ex = sb("ex", [P, QT, HPU, NK], F32)
        den = sb("den", [P, QT, HPU], F32)
        rden = sb("rden", [P, QT, HPU], F32)
        pr = sb("pr", [P, QT, HPU, NK], F32)
        pT_h = sb("pT_h", [NK, HPU, NQ], F16)
        pT_l = sb("pT_l", [NK, HPU, NQ], F16)
        oT_h = sb("oT_h", [P, PPU, NQ], F32R)
        oT_l = sb("oT_l", [P, PPU, NQ], F32R)
        x1 = sb("x1", [P, QT, D], F32)
        st2 = sb("st2", [P, QT, 6], F32)
        mv2 = sb("mv2", [P, QT, 2], F32)
        rs2 = sb("rs2", [P, QT], F32)
        ve2 = sb("ve2", [P, QT], F32)
        x2 = sb("x2", [P, QT, D], F32)
        x2T_h = sb("x2T_h", [P, KT, NQ], F32R)
        x2T_l = sb("x2T_l", [P, KT, NQ], F32R)
        th = sb("th", [P, 2, NQ], F32)
        sg = sb("sg", [P, 2, NQ], F32)
        hf = sb("hf", [P, 2, NQ], F32)
        hT_h = sb("hT_h", [P, HC, NQ], F32R)
        hT_l = sb("hT_l", [P, HC, NQ], F32R)
        am = sb("am", [P, QT], F32)
        lsc = sb("lsc", [P, QT], F32)
        linv = sb("linv", [P, QT], F32)
        q_a = sb("q_a", [P, QT, D], F32)
        q_b = sb("q_b", [P, QT, D], F32)
        q_i = sb("q_i", [P, QT, D], F16)
        qiT = sb("qiT", [P, KT, NQ], F16)
        ya = sb("ya", [P, QT, D], F32)
        y = sb("y", [P, QT, D], F32)

        SC = psum[:, 0:2, 0:HPU * NK]
        PT = psum[0:NK, 2:4, :].rearrange("p b (h q) -> p b h q", q=NQ)
        OV = psum[:, 4, :].rearrange("p (a q) -> p a q", q=NQ)
        OA = psum[:, 5, :].rearrange("p (t d) -> p t d", d=D)
        RG = [psum[:, 6 + i, :].rearrange("p (a q) -> p a q", q=NQ) for i in range(2)]

        s_late = sem("s_late")
        s_lh, s_ll = sem("s_lh"), sem("s_ll")
        s_lp = sem("s_lp")
        s_kb = [sem(f"s_kb{u}") for u in range(UNITS)]
        s_vb = [sem(f"s_vb{u}") for u in range(UNITS)]
        s_xr = sem("s_xr")
        s_y = sem("s_y")
        s_xt, s_xh, s_xl = sem("s_xt"), sem("s_xh"), sem("s_xl")
        s_q, s_qh, s_ql = sem("s_q"), sem("s_qh"), sem("s_ql")
        s_s, s_m = sem("s_s"), sem("s_m")
        s_e = sem("s_e")
        s_r, s_p = sem("s_r"), sem("s_p")
        s_t, s_ph, s_pl = sem("s_t"), sem("s_ph"), sem("s_pl")
        s_pv, s_oh, s_ol = sem("s_pv"), sem("s_oh"), sem("s_ol")
        s_oa = sem("s_oa")
        s_xb, s_x1 = sem("s_xb"), sem("s_x1")
        s_st2, s_mv2, s_ve2, s_rs2, s_x2 = (sem(f"s_{a}") for a in ("st2", "mv2", "ve2", "rs2", "x2"))
        s_xt2, s_x2h, s_x2l = sem("s_xt2"), sem("s_x2h"), sem("s_x2l")
        s_g, s_th, s_sg, s_hf, s_hh, s_hl = (sem(f"s_{a}") for a in ("g", "th", "sg", "hf", "hh", "hl"))
        s_d, s_yd = sem("s_d"), sem("s_yd")
        s_am, s_ls, s_li, s_qa, s_qb, s_qi = (sem(f"s_{a}") for a in ("am", "ls", "li", "qa", "qb", "qi"))
        s_yx, s_yq = sem("s_yx"), sem("s_yq")
        s_qt, s_qe = sem("s_qt"), sem("s_qe")
        s_a1, s_ya = sem("s_a1"), sem("s_ya")
        s_kz = sem("s_kz")

        x_src = [x.rearrange("b (t p) d -> b p t d", p=P), mid_d.rearrange("b (t p) d -> b p t d", p=P)]
        y_dst = [mid_d.rearrange("b (t p) d -> b p t d", p=P), out.rearrange("b (t p) d -> b p t d", p=P)]

        def as_f16(bank):
            return bank[:, 0, :].bitcast(F16).rearrange("p (k q) -> p k q", q=NQ)

        def batch_of(ap, b):
            return ap[bass.ds(b, 1)].rearrange("o p t d -> (o p) t d")

        def layer_of(g):
            return None if g < 0 or g >= NB else g // B

        def uses(l2, l1, l0, ln):
            out = []
            for u in range(UNITS):
                if l0 is not None and (u < UNITS - 1 or ln is not None):
                    out.append(("q", u))
                if l2 == 0:
                    out += [[("gu", 1), ("gu", 2)], [("gu", 3), ("gu", 4)], [], [("down", 0)]][u]
                if l2 == 1:
                    out += [[], [("turned_q", 0), ("down", 0), ("down", 1)], [], []][u]
                if u == 2:
                    if l0 is not None and ln is not None:
                        out.append(("turned_x", 0))
                    if l2 == 0:
                        out.append(("gu", 5))
                if u == 3:
                    if l1 == 0:
                        out.append(("turned_x2", 0))
                    if l2 == 0:
                        out.append(("down", 1))
                    if l1 == 0:
                        out.append(("gu", 0))
            return out

        def released(use, h, l2, l1):
            kind, k = use
            if kind == "q":
                return s_ql, UNITS * h + k + 2
            if kind == "turned_x":
                return s_xl, h + 2
            if kind == "turned_x2":
                return s_x2l, h
            if kind == "turned_q":
                return s_qe, h - 1 - B
            if kind == "gu":
                return s_hf, HC * (h - 1 if k == 0 else h - 2) + k + 1
            if l2 == 0:
                return s_yd, QT * (h - 2) + k + 1
            return s_ya, QT * (h - 2 - B) + k + 1

        kinds, gu0 = {}, None
        ring = [(("turned_x", 0), -1), (("q", UNITS - 1), -1)]
        place = 0
        for h in range(NB + 2):
            ls = tuple(layer_of(h + d) for d in (-2, -1, 0, 1))
            plan, here = {}, []
            for q, use in enumerate(uses(*ls)):
                before = (ring + here)[-2]
                plan[use] = ((place + q) % 2, before)
                here.append((use, 0))
            place += len(here)
            ring = [(use, d - 1) for use, d in (ring + here)[-2:]]
            kinds[h] = (ls, plan, gu0)
            gu0 = plan[("gu", 0)][0] if ("gu", 0) in plan else None
        for loop in (range(3, B - 1), range(B + 3, NB - 1)):
            assert all(kinds[h] == kinds[loop[0]] for h in loop)

        def bodies(eng, body):
            def one(h, like):
                ls, plan, gu0 = kinds[like]
                body(h, plan, like, gu0, *ls)

            for first, last in ((3, B - 1), (B + 3, NB - 1)):
                for h in range(first - 3, first):
                    one(h, h)
                with eng.Fori(first, last) as h:
                    one(h, first)
                one(last, last)
            one(NB, NB)
            one(NB + 1, NB + 1)

        with nc.Block() as block:
            @block.sync
            def _(sp):
                def load_keys(u, at, l):
                    cols = bass.ds(at, NK)
                    for part in range(2):
                        for a in range(2):
                            src = keys_d[l][part, u * PPU:(u + 1) * PPU, a * DH:(a + 1) * DH].rearrange(
                                "m p k -> p m k")[:, :, cols]
                            sp.dma_start(kb[u][a * DH:(a + 1) * DH, part, :, a * NK:(a + 1) * NK],
                                         src).then_inc(s_kb[u], 16)

                def load_values(u, at, l):
                    src = vals_d[l].rearrange("r k c -> k r c")[bass.ds(at, NK), :,
                                                               u * HPU * DH:(u + 1) * HPU * DH]
                    sp.dma_start(vb[u][:, :, :], src).then_inc(s_vb[u], 16)

                def load_x(dst, s, b, l):
                    sp.dma_start(dst, batch_of(x_src[l], b)).then_inc(s, 16)

                def ready(e):
                    return e if isinstance(e, int) else sp.snap(e)

                def load_late():
                    for k, item in enumerate(late_items):
                        d, src = late_raw[:, k, :], item[0]
                        if len(src.shape) == 3:
                            d = d.rearrange("p (t d) -> p t d", d=D)
                        sp.dma_start(d, src).then_inc(s_late, 16)

                sp.sem_inc(s_y, 16)
                sp.wait_ge(s_kz, UNITS)
                for u in range(UNITS):
                    load_keys(u, 0, 0)
                for u in range(UNITS - 2):
                    load_values(u, 0, 0)

                def body(h, plan, like, gu0, l2, l1, l0, ln):
                    n = UNITS * h
                    if l2 is not None:
                        b_out = ready(h - 2 - l2 * B)
                    if l0 is not None:
                        b_own = ready(h - l0 * B)
                        at_own = ready((h - l0 * B) * NK)
                    if ln is not None:
                        b_next = ready(h + 1 - ln * B)
                        at_next = ready((h + 1 - ln * B) * NK)
                    for u in range(UNITS):
                        if l0 is not None and ln is not None:
                            if u == 0:
                                if ln == 1:
                                    sp.wait_ge(s_y, 16 * (h + 3 - B))
                                sp.wait_ge(s_xn, QT * (h + 1))
                                load_x(x_in[:, :, :], s_x, b_next, ln)
                        if l0 is not None and u < 2:
                            if l1 is not None:
                                sp.wait_ge(s_pv, n + u - 1)
                            load_values(u + 2, at_own, l0)
                        if l0 is not None and ln is not None:
                            sp.wait_ge(s_s, n + u + 1)
                            load_keys(u, at_next, ln)
                            if u >= 2:
                                sp.wait_ge(s_pv, n + u - 1)
                                load_values(u - 2, at_next, ln)
                        if u == 3 and l0 is not None:
                            if l0 == 1:
                                sp.wait_ge(s_y, 16 * (h + 2 - B))
                            if l1 is not None:
                                sp.wait_ge(s_x1, h)
                            load_x(x_res[:, :, :], s_xr, b_own, l0)
                        if like == 0 and u == 3:
                            load_late()
                        if (u == 3 and l2 == 0) or (u == 2 and l2 == 1):
                            sp.wait_ge(*((s_yd, QT * (h - 1)) if l2 == 0 else (s_yq, h - 1 - B)))
                            sp.dma_start(batch_of(y_dst[l2], b_out), y[:, :, :]).then_inc(s_y, 16)

                bodies(sp, body)
                sp.wait_ge(s_y, 16 * (NB + 1))

            @block.tensor
            def _(pe):
                def turn(dst, src):
                    for k in range(KT):
                        for t in range(QT):
                            last = pe.transpose(dst[:, k, t * P:(t + 1) * P], src[:, t, k * P:(k + 1) * P],
                                                (ident if src.dtype == F32 else ident16)[:, :])
                    return last

                def scores(n, u, k_need):
                    pe.wait_ge(s_ql, n + 1)
                    pe.wait_ge(s_kb[u], k_need)
                    for t in range(QT):
                        if not (isinstance(n, int) and n == 0):
                            pe.wait_ge(s_e, QT * (n - 1) + t + 1)
                        for a in range(PPU):
                            o = SC[:, t, a * 2 * NK:(a + 1) * 2 * NK]
                            ts = slice(t * P, (t + 1) * P)
                            for q, (w, part) in enumerate(((qT_h, 0), (qT_h, 1), (qT_l, 0))):
                                last = pe.matmul(o, w[:, a, ts], kb[u][:, part, a, :], start=(q == 0), stop=(q == 2))
                    last.then_inc(s_s, 1)

                def turn_probabilities(n):
                    pe.wait_ge(s_p, n + 1)
                    pe.wait_ge(s_pl, 2 * n)
                    for a in range(PPU):
                        for b in range(2):
                            for t in range(QT):
                                last = pe.transpose(PT[:, a, b, t * P:(t + 1) * P], pr[:, t, 2 * a + b, :],
                                                    ident[:, :])
                        last.then_inc(s_t, 1)

                def queries(u, l, o):
                    for a in range(PPU):
                        w = slice((u * PPU + a) * P, (u * PPU + a + 1) * P)
                        terms = [(ww, xx, k) for k in range(KT) for ww, xx in
                                 ((wq_h[l], xT_h), (wq_h[l], xT_l), (wq_l[l], xT_h))]
                        for q, (ww, xx, k) in enumerate(terms):
                            last = pe.matmul(o[:, a, :], ww[:, k, w], xx[:, k, :], start=(q == 0),
                                             stop=(q == len(terms) - 1))
                    last.then_inc(s_q, 1)

                def project(n, u, l):
                    pe.wait_ge(s_ol, n + 1)
                    for t in range(QT):
                        for a in range(PPU):
                            ts, k = slice(t * P, (t + 1) * P), u * PPU + a
                            for q, (oo, ww) in enumerate(((oT_h, wo_h[l]), (oT_l, wo_h[l]), (oT_h, wo_l[l]))):
                                first = u == 0 and t == 0 and a == 0 and q == 0
                                last = pe.matmul(OA[:, t, :], oo[:, a, ts], ww[:, k, :], start=first,
                                                 stop=(u == UNITS - 1 and a == PPU - 1 and q == 2),
                                                 skip_group_check=True)
                    if u == UNITS - 1:
                        last.then_inc(s_oa, 1)

                def weigh_values(n, u, v_need):
                    pe.wait_ge(s_vb[u], v_need)
                    if not (isinstance(n, int) and n == 0):
                        pe.wait_ge(s_ol, n)
                    for a in range(PPU):
                        pe.wait_ge(s_pl, 2 * n + a + 1)
                        for q, (part, pp) in enumerate(((0, pT_h), (0, pT_l), (1, pT_h))):
                            for b in range(2):
                                hd = 2 * a + b
                                last = pe.matmul(OV[b * DH:(b + 1) * DH, a, :], vb[u][:, part, hd * DH:(hd + 1) * DH],
                                                 pp[:, hd, :], start=(q == 0), stop=(q == 2))
                    last.then_inc(s_pv, 1)

                def gate_up(c, o):
                    for a, w in ((0, wgT), (1, wuT)):
                        terms = [(k, xx) for k in range(KT) for xx in (x2T_h, x2T_l)]
                        for q, (k, xx) in enumerate(terms):
                            last = pe.matmul(o[:, a, :], w[:, k, c * P:(c + 1) * P], xx[:, k, :], start=(q == 0),
                                             stop=(q == len(terms) - 1))
                    last.then_inc(s_g, 1)

                def down(t, o):
                    terms = [(c, hh) for c in range(HC) for hh in (hT_h, hT_l)]
                    for q, (c, hh) in enumerate(terms):
                        last = pe.matmul(o[:, 0, :], hh[:, c, t * P:(t + 1) * P], wdT[:, c, :], start=(q == 0),
                                         stop=(q == len(terms) - 1))
                    last.then_inc(s_d, 1)

                def quantised(t, o):
                    for k in range(KT):
                        last = pe.matmul(o[:, 0, :], qiT[:, k, t * P:(t + 1) * P], rhs_q[:, k, :], start=(k == 0),
                                         stop=(k == KT - 1))
                    last.then_inc(s_a1, 1)

                pe.wait_ge(s_xn, QT)
                turn(RG[0], xn).then_inc(s_xt, 1)
                pe.wait_ge(s_xl, 1)
                queries(0, 0, RG[1])

                def body(h, plan, like, gu0, l2, l1, l0, ln):
                    n = UNITS * h

                    def bank(*use):
                        where, (before, d) = plan[use]
                        ls = kinds[like + d][0] if like + d >= 0 else (None, None, None, 0)
                        pe.wait_ge(*released(before, h + d, ls[0], ls[1]))
                        return RG[where]

                    if like == B - 1:
                        pe.wait_ge(s_ll, len(late_items) // 2)
                        pe.wait_ge(s_lp, len(late_items) // 2)
                    for u in range(UNITS):
                        one, two, three = (l0 if u >= d else l1 for d in (1, 2, 3))
                        if l0 is not None:
                            scores(n + u, u, 64 * (h + 1))
                        if ("q", u) in plan:
                            if u == UNITS - 1:
                                pe.wait_ge(s_xl, h + 2)
                            queries((u + 1) % UNITS, l0 if u < UNITS - 1 else ln, bank("q", u))
                        if three is not None:
                            if u == 3 and l1 is not None:
                                pe.wait_ge(s_x1, h)
                            project(n + u - 3, (u - 3) % UNITS, three)
                        if l2 == 0 and u < 2:
                            gate_up(2 * u + 1, bank("gu", 2 * u + 1))
                        if ("turned_x", 0) in plan and u == 2:
                            pe.wait_ge(s_xn, QT * (h + 2))
                            turn(bank("turned_x", 0), xn).then_inc(s_xt, 1)
                        if two is not None:
                            weigh_values(n + u - 2, (u - 2) % UNITS, 16 * (h if u < 2 else h + 1))
                        if l2 == 0 and u == 3:
                            pe.wait_ge(s_hl, HC * (h - 1))
                            down(0, bank("down", 0))
                        if l2 == 1 and u == 1:
                            pe.wait_ge(s_qi, h - 1 - B)
                            turn(as_f16(bank("turned_q", 0)), q_i).then_inc(s_qt, 1)
                        if l1 == 0 and u == 3:
                            pe.wait_ge(s_x2, QT * h)
                            turn(bank("turned_x2", 0), x2).then_inc(s_xt2, 1)
                        if one is not None:
                            turn_probabilities(n + u - 1)
                        if l2 == 0 and u < 3:
                            c = (2, 4, 5)[u]
                            gate_up(c, bank("gu", c))
                        if l2 == 1 and u == 1:
                            pe.wait_ge(s_qe, h - 1 - B)
                            for t in range(QT):
                                quantised(t, bank("down", t))
                        if l2 == 0 and u == 3:
                            down(1, bank("down", 1))
                        if l1 == 0 and u == 3:
                            pe.wait_ge(s_x2l, h)
                            gate_up(0, bank("gu", 0))

                bodies(pe, body)

            @block.scalar
            def _(act):
                def high(dst, src):
                    return act.activation(dst, src, ACT.Copy)

                act.wait_ge(s_xt, 1)
                high(xT_h[:, :, :], RG[0]).then_inc(s_xh, 1)
                act.wait_ge(s_q, 1)
                high(qT_h[:, :, :], RG[1]).then_inc(s_qh, 1)

                def body(h, plan, like, gu0, l2, l1, l0, ln):
                    n = UNITS * h

                    def bank(*use):
                        return RG[plan[use][0]]

                    def tanh_gate(c, b):
                        act.wait_ge(s_g, HC * b + c + 1)
                        act.activation(th[:, c % 2, :], bank("gu", c)[:, 0, :], ACT.Tanh,
                                       scale=G_SCALE).then_inc(s_th, 1)

                    def high_hidden(c):
                        act.wait_ge(s_hf, HC * (h - 2) + c + 1)
                        high(hT_h[:, c, :], hf[:, c % 2, :]).then_inc(s_hh, 1)

                    def exponentials(n, t):
                        for b in range(HPU):
                            last = act.activation(ex[:, t, b, :], SC[:, t, b * NK:(b + 1) * NK], ACT.Exp,
                                                  bias=nmax[:, t, b:b + 1], accum_out=den[:, t, b:b + 1])
                        last.then_inc(s_e, 1)

                    for u in range(UNITS):
                        one, two = (l0 if u >= d else l1 for d in (1, 2))
                        if l0 is not None:
                            if not (isinstance(n, int) and n + u == 0):
                                act.wait_ge(s_p, n + u)
                            act.wait_ge(s_m, n + u + 1)
                            exponentials(n + u, 0)
                        if l2 == 0:
                            high_hidden((0, 2, 4, 5)[u])
                        if l2 == 1 and u == 1:
                            act.wait_ge(s_qb, h - 1 - B)
                            act.activation(q_i[:, :, :], q_b[:, :, :], ACT.Copy, bias=-MAGIC).then_inc(s_qi, 1)
                        if ("q", u) in plan:
                            act.wait_ge(s_q, n + u + 2)
                            high(qT_h[:, :, :], bank("q", u)).then_inc(s_qh, 1)
                        if l0 is not None:
                            exponentials(n + u, 1)
                        if l2 == 0 and u < 2:
                            tanh_gate(2 * u + 1, h - 2)
                        if ("turned_x", 0) in plan and u == 2:
                            act.wait_ge(s_xt, h + 2)
                            high(xT_h[:, :, :], bank("turned_x", 0)).then_inc(s_xh, 1)
                        if two is not None:
                            act.wait_ge(s_pv, n + u - 1)
                            high(oT_h[:, :, :], OV).then_inc(s_oh, 1)
                        if l1 == 0 and u == 3:
                            act.wait_ge(s_xt2, h)
                            high(x2T_h[:, :, :], bank("turned_x2", 0)).then_inc(s_x2h, 1)
                        if l2 == 0 and u < 2:
                            high_hidden(2 * u + 1)
                        if one is not None:
                            for a in range(PPU):
                                act.wait_ge(s_t, 2 * (n + u - 1) + a + 1)
                                high(pT_h[:, 2 * a:2 * a + 2, :], PT[:, a]).then_inc(s_ph, 1)
                        if l2 == 1 and u == 0:
                            act.wait_ge(s_li, h - 1 - B)
                            for t in range(QT):
                                act.activation(q_a[:, t, :], x2[:, t, :], ACT.Copy, scale=linv[:, t:t + 1],
                                               bias=MAGIC).then_inc(s_qa, 1)
                        if l2 == 0 and u < 3:
                            tanh_gate((2, 4, 5)[u], h - 2)
                        if l1 == 0 and u == 3:
                            tanh_gate(0, h - 1)
                        if like == 1:
                            _, hi, lo, scale = late_items[u]
                            act.wait_ge(s_late, 16 * len(late_items))
                            act.activation(hi, late_raw[:, u, :], ACT.Copy, scale=scale).then_inc(s_lh, 1)

                bodies(act, body)

            @block.vector
            def _(dve):
                def low(dst, src, hi):
                    if hi.dtype == F32R:
                        hi = hi.bitcast(F32)
                    return dve.tensor_tensor(dst, src, hi, ALU.subtract)

                def stats(src, st, s_done):
                    for t in range(QT):
                        dve.bn_stats(st[:, t, :], src[:, t, :]).then_inc(s_done, 1)

                def aggregate(st, mv, s_done):
                    for t in range(QT):
                        dve.bn_aggr(mv[:, t, :], st[:, t, :]).then_inc(s_done, 1)

                def normalise(dst, src, mv, rs, s_rs_, s_done, g):
                    dve.wait_ge(s_rs_, g + 1)
                    for t in range(QT):
                        dve.tensor_scalar(dst[:, t, :], src[:, t, :], mv[:, t, 0:1], rs[:, t:t + 1],
                                          ALU.subtract, ALU.mult).then_inc(s_done, 1)

                dve.wait_ge(s_xh, 1)
                low(xT_l[:, :, :], RG[0], xT_h[:, :, :]).then_inc(s_xl, 1)
                dve.wait_ge(s_qh, 1)
                low(qT_l[:, :, :], RG[1], qT_h[:, :, :]).then_inc(s_ql, 1)

                def body(h, plan, like, gu0, l2, l1, l0, ln):
                    n = UNITS * h

                    def bank(*use):
                        return RG[plan[use][0]]

                    def hidden(c):
                        k = HC * (h - 2) + c
                        o = RG[gu0] if c == 0 else bank("gu", c)
                        dve.wait_ge(s_th, k + 1)
                        dve.scalar_tensor_tensor(out=sg[:, c % 2, :], in0=th[:, c % 2, :], scalar=1.0,
                                                 in1=o[:, 0, :], op0=ALU.add, op1=ALU.mult).then_inc(s_sg, 1)
                        dve.wait_ge(s_sg, k + 1)
                        if c >= 2:
                            dve.wait_ge(s_hl, k - 1)
                        dve.tensor_tensor(hf[:, c % 2, :], o[:, 1, :], sg[:, c % 2, :], ALU.mult).then_inc(s_hf, 1)

                    def out_rows(t):
                        dve.wait_ge(s_d, QT * (h - 2) + t + 1)
                        dve.wait_ge(s_yx, h - 1)
                        dve.scalar_tensor_tensor(out=y[:, t, :], in0=bank("down", t)[:, 0, :], scalar=FFN_SCALE,
                                                 in1=y[:, t, :], op0=ALU.mult, op1=ALU.add).then_inc(s_yd, 1)

                    def descale(t):
                        dve.wait_ge(s_a1, QT * (h - 2 - B) + t + 1)
                        dve.scalar_tensor_tensor(out=ya[:, t, :], in0=bank("down", t)[:, 0, :],
                                                 scalar=lsc[:, t:t + 1], in1=rhs_sb[:, :], op0=ALU.mult,
                                                 op1=ALU.mult).then_inc(s_ya, 1)

                    for u in range(UNITS):
                        two = l0 if u >= 2 else l1
                        if l0 is not None:
                            dve.wait_ge(s_s, n + u + 1)
                            dve.tensor_reduce(nmax[:, :, :], SC.rearrange("p t (h k) -> p t h k", k=NK), AX_X,
                                              ALU.max, negate=True).then_inc(s_m, 1)
                        if l2 == 0:
                            hidden((0, 2, 4, 5)[u])
                        if l0 is not None and ln is not None and u == 2:
                            normalise(xn, x_in, mv1, rs1, s_rs, s_xn, h + 1)
                        if l2 == 1 and u == 1:
                            dve.wait_ge(s_qa, QT * (h - 1 - B))
                            dve.tensor_scalar(q_b[:, :, :], q_a[:, :, :], MAGIC - INT8_MAX, MAGIC + INT8_MAX,
                                              ALU.max, ALU.min).then_inc(s_qb, 1)
                        if two is not None:
                            for a in range(PPU):
                                dve.wait_ge(s_ph, 2 * (n + u - 2) + a + 1)
                                low(pT_l[:, 2 * a:2 * a + 2, :], PT[:, a],
                                    pT_h[:, 2 * a:2 * a + 2, :]).then_inc(s_pl, 1)
                        if l0 is not None and ln is not None and u == 1:
                            dve.wait_ge(s_x, 16 * (h + 2))
                            stats(x_in, st1, s_st)
                            dve.wait_ge(s_st, QT * (h + 2))
                        if l2 == 1 and u == 0:
                            normalise(x2, x1, mv2, rs2, s_rs2, s_x2, h - 2)
                        if l1 == 1 and u == 3:
                            dve.wait_ge(s_x1, h)
                            stats(x1, st2, s_st2)
                            dve.wait_ge(s_st2, QT * h)
                        if l1 == 0 and u == 3:
                            normalise(x2, x1, mv2, rs2, s_rs2, s_x2, h - 1)
                        if l2 == 1 and u == 1:
                            dve.wait_ge(s_qt, h - 1 - B)
                            dve.tensor_copy(qiT[:, :, :], as_f16(bank("turned_q", 0))).then_inc(s_qe, 1)
                        if ("q", u) in plan:
                            dve.wait_ge(s_qh, n + u + 2)
                            low(qT_l[:, :, :], bank("q", u), qT_h[:, :, :]).then_inc(s_ql, 1)
                        if l1 == 1 and u == 3:
                            aggregate(st2, mv2, s_mv2)
                        if l0 is not None and ln is not None and u == 1:
                            aggregate(st1, mv1, s_mv)
                        if l2 == 1 and u == 0:
                            g = h - 2 - B
                            dve.wait_ge(s_x2, QT * (h - 1))
                            dve.tensor_reduce(am[:, :], x2[:, :, :], AX_X, ALU.max,
                                              apply_absolute_value=True).then_inc(s_am, 1)
                            dve.wait_ge(s_am, g + 1)
                            dve.tensor_scalar(lsc[:, :], am[:, :], 1e-12, 1.0 / INT8_MAX, ALU.max,
                                              ALU.mult).then_inc(s_ls, 1)
                            dve.wait_ge(s_ls, g + 1)
                            dve.reciprocal(linv[:, :], lsc[:, :]).then_inc(s_li, 1)
                        if l0 is not None:
                            dve.wait_ge(s_e, QT * (n + u + 1))
                            dve.reciprocal(rden[:, :, :], den[:, :, :]).then_inc(s_r, 1)
                        if l2 == 0 and u < 2:
                            hidden(2 * u + 1)
                        if l1 is not None and u == 2:
                            dve.wait_ge(s_oa, h)
                            dve.wait_ge(s_xb, h)
                            if l2 == 0:
                                dve.wait_ge(s_yx, h - 1)
                            elif l2 == 1:
                                dve.wait_ge(s_yq, h - 1 - B)
                            dve.tensor_tensor(x1[:, :, :], OA, x_res[:, :, :], ALU.add).then_inc(s_x1, 1)
                        if l2 == 0 and u == 3:
                            out_rows(0)
                        if ("turned_x", 0) in plan and u == 2:
                            dve.wait_ge(s_xh, h + 2)
                            low(xT_l[:, :, :], bank("turned_x", 0), xT_h[:, :, :]).then_inc(s_xl, 1)
                        if l1 == 0 and u == 2:
                            dve.wait_ge(s_x1, h)
                            stats(x1, st2, s_st2)
                            dve.wait_ge(s_st2, QT * h)
                        if two is not None:
                            dve.wait_ge(s_oh, n + u - 1)
                            low(oT_l[:, :, :], OV, oT_h[:, :, :]).then_inc(s_ol, 1)
                        if l1 == 0 and u == 2:
                            aggregate(st2, mv2, s_mv2)
                        if l2 == 1 and u == 1:
                            for t in range(QT):
                                descale(t)
                        if l1 == 0 and u == 3:
                            dve.wait_ge(s_x2h, h)
                            low(x2T_l[:, :, :], bank("turned_x2", 0), x2T_h[:, :, :]).then_inc(s_x2l, 1)
                        if l2 == 0 and u == 3:
                            out_rows(1)
                        if like == 2 and u % 2 == 0:
                            _, hi, lo, scale = late_items[u]
                            dve.wait_ge(s_lh, u + 1)
                            dve.scalar_tensor_tensor(out=lo, in0=late_raw[:, u, :], scalar=scale,
                                                     in1=hi.bitcast(F32), op0=ALU.mult,
                                                     op1=ALU.subtract).then_inc(s_ll, 1)

                bodies(dve, body)

            @block.gpsimd
            def _(pool):
                for u in range(UNITS):
                    pool.memset(kb[u][:, :, :, :], 0.0).then_inc(s_kz, 1)

                def inverse_deviation(mv, ve, rs, s_mv_, s_ve_, s_rs_, g):
                    pool.wait_ge(s_mv_, QT * (g + 1))
                    pool.tensor_tensor(ve[:, :], mv[:, :, 1], eps[:, :], ALU.add).then_inc(s_ve_, 1)
                    pool.wait_ge(s_ve_, g + 1)
                    pool.tensor_tensor(rs[:, :], ve[:, :], half_neg[:, :], ALU.pow).then_inc(s_rs_, 1)

                def body(h, plan, like, gu0, l2, l1, l0, ln):
                    n = UNITS * h

                    def low_hidden(c):
                        pool.wait_ge(s_hh, HC * (h - 2) + c + 1)
                        pool.tensor_tensor(hT_l[:, c, :], hf[:, c % 2, :], hT_h[:, c, :].bitcast(F32),
                                           ALU.subtract).then_inc(s_hl, 1)

                    for u in range(UNITS):
                        if l1 == 0 and u == 3:
                            inverse_deviation(mv2, ve2, rs2, s_mv2, s_ve2, s_rs2, h - 1)
                        if l2 == 0:
                            low_hidden((0, 2, 4, 5)[u])
                        if like == 2 and u % 2 == 1:
                            _, hi, lo, scale = late_items[u]
                            pool.wait_ge(s_lh, u + 1)
                            pool.tensor_tensor(lo, late_raw[:, u, :], hi.bitcast(F32), ALU.subtract).then_inc(s_lp, 1)
                        if l2 == 1 and u == 2:
                            pool.wait_ge(s_y, 16 * (h - 1))
                            pool.wait_ge(s_ya, QT * (h - 1 - B))
                            pool.tensor_tensor(y[:, :, :], ya[:, :, :], x1[:, :, :], ALU.add).then_inc(s_yq, 1)
                        if l1 == 1 and u == 3:
                            inverse_deviation(mv2, ve2, rs2, s_mv2, s_ve2, s_rs2, h - 1)
                        if l0 is not None:
                            pool.wait_ge(s_r, n + u + 1)
                            if not (isinstance(n, int) and n + u == 0):
                                pool.wait_ge(s_t, 2 * (n + u))
                            r = rden[:, :, :].unsqueeze(3).to_broadcast([P, QT, HPU, NK])
                            pool.tensor_tensor(pr[:, :, :, :], ex[:, :, :, :], r, ALU.mult).then_inc(s_p, 1)
                        if u == 1 and l0 is not None and ln is not None:
                            inverse_deviation(mv1, ve1, rs1, s_mv, s_ve, s_rs, h + 1)
                        if u == 0 and l1 is not None:
                            pool.wait_ge(s_xr, 16 * h)
                            bias = bo_b[l1][:, :].unsqueeze(1).to_broadcast([P, QT, D])
                            pool.tensor_tensor(x_res[:, :, :], x_res[:, :, :], bias, ALU.add).then_inc(s_xb, 1)
                        if l2 == 0 and u == 1:
                            pool.wait_ge(s_y, 16 * (h - 1))
                        if l2 == 0 and u < 2:
                            low_hidden(2 * u + 1)
                        if l2 == 0 and u == 1:
                            pool.tensor_copy(y[:, :, :], x1[:, :, :]).then_inc(s_yx, 1)

                bodies(pool, body)


_INS = ['x', 'ctx_768', 'L0_xattn_Wq', 'L0_xattn_Wk', 'L0_xattn_Wv', 'L0_xattn_Wo', 'L0_xattn_bo',
        'L0_ffn_w_gate', 'L0_ffn_w_up', 'L0_ffn_w_down', 'L1_xattn_Wq', 'L1_xattn_Wk', 'L1_xattn_Wv',
        'L1_xattn_Wo', 'L1_xattn_bo', 'L1_ffn_rhs']
_OUTS = [((32, 256, 256), 'float32')]


def kernel(**inputs):
    import numpy as _np
    import concourse.bacc as _bacc
    from concourse import mybir as _mybir
    from concourse.bass_utils import run_bass_kernel_spmd as _run

    nc = _bacc.Bacc("TRN2", target_bir_lowering=False, num_devices=1)
    arrays, args = {}, []
    for name in _INS:
        a = _np.ascontiguousarray(inputs[name])
        arrays[f"in_{name}_dram"] = a
        args.append(nc.dram_tensor(f"in_{name}_dram", a.shape, _mybir.dt.from_np(a.dtype), kind="ExternalInput").ap())
    for i, (shape, dtype) in enumerate(_OUTS):
        dt = _mybir.dt.from_np(_np.dtype(dtype))
        args.append(nc.dram_tensor(f"out_{i}_dram", shape, dt, kind="ExternalOutput").ap())
    xattn_ffn_kernel(nc, *args)
    r = _run(nc, [arrays], core_ids=[0])
    return r.results[0]["out_0_dram"]
```
